# Optimizing a Trainium2 kernel written in Bass

```python
import numpy as np
import jax
import jax.numpy as jnp

def _softmax(x, axis=-1):
    return jax.nn.softmax(x, axis=axis)

def _gelu(x):
    return jax.nn.gelu(x, approximate=True)

def _silu(x):
    return jax.nn.silu(x)

def _sigmoid(x):
    return jax.nn.sigmoid(x)

def _layernorm(x, axis=-1, eps=1e-05):
    m = jnp.mean(x, axis=axis, keepdims=True)
    v = jnp.var(x, axis=axis, keepdims=True)
    return (x - m) / jnp.sqrt(v + eps)

def _scatter_add(tgt, idx, src, axis=0):
    return tgt.at[idx].add(src)

def _segment_sum(src, seg, n):
    return jax.ops.segment_sum(src, seg, n)
kernel_name = 'mk_adj_preln_d2_adj_r2_d396db'

def setup_inputs(seed: int=0):
    np.random.seed(seed)
    _w = jnp.asarray

    def _rec_inputs():
        import jax
        import jax.numpy as jnp
        _gk = jax.random.key(seed)
        x = -0.000929 + 1 * jax.random.normal(jax.random.fold_in(_gk, 1), (4096, 128), jnp.float32)
        _a = jax.random.bernoulli(jax.random.fold_in(_gk, 2), 0.00195312, (4096, 4096))
        _a = jnp.logical_or(_a, jnp.swapaxes(_a, -1, -2))
        _a = jnp.logical_or(_a, jnp.eye(4096, dtype=bool))
        _af = _a.astype(jnp.float32)
        _af = _af * jax.random.uniform(jax.random.fold_in(_gk, 3), (4096, 4096), jnp.float32, 0.05, 1)
        adj = _af
        return (x, adj)
    x, adj = _rec_inputs()

    def _L0_gnn_setup():
        import jax, jax.numpy as jnp
        import numpy as np
        N = 4096
        D = 128

        def _xavier(key, shape):
            fan_in, fan_out = shape
            limit = float(np.sqrt(6.0 / (fan_in + fan_out)))
            return jax.random.uniform(key, shape, jnp.float32, -limit, limit)
        key = jax.random.key(seed)
        kH, kA, k1, k2, k3, k4 = jax.random.split(key, 6)
        return {'H': jax.random.normal(kH, (N, D), jnp.float32), 'adj': jax.random.uniform(kA, (N, N), jnp.float32), 'W_l': _xavier(k1, (D, D)), 'W_r': _xavier(k2, (D, D)), 'W_h': _xavier(k3, (D, D)), 'W_g': _xavier(k4, (D, D)), 'gamma': jnp.zeros((1,), jnp.float32)}
    _L0_gnn_all = _L0_gnn_setup()
    _L0_gnn_in = {k: v for k, v in _L0_gnn_all.items() if k in ('W_l', 'W_r', 'W_h', 'W_g', 'gamma')}
    del _L0_gnn_all

    def _L1_gnn_setup():
        import jax, jax.numpy as jnp
        import numpy as np
        IN_F, OUT_F = (128, 128)
        R, LEV, N = (2, 2, 4096)
        JD = (R - 1) * LEV + 1
        key = jax.random.key(seed)
        ks = jax.random.split(key, 7)
        x = jax.random.normal(ks[0], (N, IN_F), dtype=jnp.float32)
        d_list = jax.random.uniform(ks[1], (JD, N), dtype=jnp.float32)
        U = jax.random.normal(ks[2], (N, N), dtype=jnp.float32)
        Vt = jax.random.normal(ks[3], (N, N), dtype=jnp.float32)
        bound = float(np.sqrt(6.0 / (IN_F + OUT_F)))
        weight = jax.random.uniform(ks[4], (IN_F, OUT_F), dtype=jnp.float32, minval=-bound, maxval=bound)
        filt = jax.random.uniform(ks[5], (JD, N), dtype=jnp.float32, minval=0.9, maxval=1.1)
        bias = jnp.zeros((OUT_F,), dtype=jnp.float32)
        return {'x': x, 'd_list': d_list, 'U': U, 'Vt': Vt, 'weight': weight, 'filt': filt, 'bias': bias}
    _L1_gnn_all = _L1_gnn_setup()
    _L1_gnn_in = {k: v for k, v in _L1_gnn_all.items() if k in ('d_list', 'weight', 'filt', 'bias')}
    del _L1_gnn_all
    return {'x': x, 'adj': adj, 'L0_gnn_W_l': _L0_gnn_in['W_l'], 'L0_gnn_W_r': _L0_gnn_in['W_r'], 'L0_gnn_W_h': _L0_gnn_in['W_h'], 'L0_gnn_W_g': _L0_gnn_in['W_g'], 'L0_gnn_gamma': _L0_gnn_in['gamma'], 'L1_gnn_d_list': _L1_gnn_in['d_list'], 'L1_gnn_weight': _L1_gnn_in['weight'], 'L1_gnn_filt': _L1_gnn_in['filt'], 'L1_gnn_bias': _L1_gnn_in['bias']}

def reference(x, adj, L0_gnn_W_l, L0_gnn_W_r, L0_gnn_W_h, L0_gnn_W_g, L0_gnn_gamma, L1_gnn_d_list, L1_gnn_weight, L1_gnn_filt, L1_gnn_bias):
    import jax
    import jax.numpy as jnp

    def _L0_gnn_ref(H, adj, W_l, W_r, W_h, W_g, gamma):
        import jax, jax.numpy as jnp
        import numpy as np
        N = 4096
        D = 128

        def _xavier(key, shape):
            fan_in, fan_out = shape
            limit = float(np.sqrt(6.0 / (fan_in + fan_out)))
            return jax.random.uniform(key, shape, jnp.float32, -limit, limit)
        H_l = H @ W_l
        H_r = H @ W_r
        S = H_l @ H_r.T
        beta = jax.nn.softmax(S, axis=-1)
        B = beta @ H
        O = B @ W_h @ W_g
        return adj @ H + gamma * O

    def _L1_gnn_ref(x, d_list, U, Vt, weight, filt, bias):
        import jax, jax.numpy as jnp
        import numpy as np
        IN_F, OUT_F = (128, 128)
        R, LEV, N = (2, 2, 4096)
        JD = (R - 1) * LEV + 1
        xw = x @ weight
        Vxw = Vt @ xw
        scale = jnp.sum(d_list * filt * d_list, axis=0)
        out = U @ (scale[:, None] * Vxw)
        return out + bias
    h = jnp.maximum(_layernorm(x, axis=-1), 0.0)
    x = x + _L0_gnn_ref(h, adj, L0_gnn_W_l, L0_gnn_W_r, L0_gnn_W_h, L0_gnn_W_g, L0_gnn_gamma)
    h = jnp.maximum(_layernorm(x, axis=-1), 0.0)
    x = x + _L1_gnn_ref(h, L1_gnn_d_list, adj, adj, L1_gnn_weight, L1_gnn_filt, L1_gnn_bias)
    return x

_drawn_inputs = setup_inputs


def setup_inputs(seed=0):
    import zlib

    import numpy as np

    out = dict(_drawn_inputs(seed))
    spreads = {'L1_gnn_bias': (0.0, 0.1)}
    factors = {}
    for name, (base, spread) in spreads.items():
        noise = np.random.default_rng([zlib.crc32(name.encode()), seed]).standard_normal(out[name].shape)
        drawn = base * np.exp(spread * noise) if base else spread * noise
        out[name] = jnp.asarray(drawn.astype(out[name].dtype))
    for name, factor in factors.items():
        out[name] = (out[name] * factor).astype(out[name].dtype)
    return out
```

```python
import concourse.bass as bass
from concourse import mybir
from contextlib import ExitStack


def preln_attention_graph_kernel(nc, x, adj, w_l, w_r, w_h, w_g, gamma, d_list, weight, filt, bias, out):
    f32, f32r = mybir.dt.float32, mybir.dt.float32r
    ALU, ACT, AX = mybir.AluOpType, mybir.ActivationFunctionType, mybir.AxisListType

    N, D = x.shape
    P = 128
    SQ = 32
    NQ = P // SQ
    SEG = N // NQ
    TILES = N // P
    EPS = 1e-5

    ROWS = 512
    CHUNKS = N // ROWS
    BLOCKS = ROWS // SQ
    CT = ROWS // P
    UT = 4
    UNITS = TILES // UT
    UE = UT * ROWS
    LU = 2
    LOADS = UNITS // LU
    NT, NS, NA = 4, 4, 2
    LOAD_INC = 16 * NQ
    POOL_TILES = (3, 2, 3, 3, 2, 3, 3, 2)
    PASSES = 3

    QR = 256
    QCH = N // QR
    QT = QR // P
    SG = 1024
    SUNITS = QT * (N // SG)
    PK = 2
    PUNITS = TILES // PK
    NPT = 4

    ctx = ExitStack()
    with ctx:
        def sb(name, shape, dt=f32):
            return ctx.enter_context(nc.sbuf_tensor(name, shape, dt))

        def sem(name):
            return ctx.enter_context(nc.semaphore(name))

        stat_hi = sb("stat_hi", [P, TILES, D], f32r)
        stat_lo = sb("stat_lo", [P, TILES, D], f32r)
        resid = sb("resid", [P, TILES, D])
        yT = sb("yT", [P, N])
        split = sb("split", [P, NS * 2 * UE], f32r)
        raw = sb("raw", [P, 2 * QT * N])
        keyT_hi = split[:, 0:N]
        keyT_lo = split[:, N:2 * N]
        pt0 = 2 * N
        probT = split[:, pt0:pt0 + NPT * PK * 2 * QR].rearrange("p (n k h r) -> p n k h r", n=NPT, k=PK, h=2)
        q0 = pt0 + NPT * PK * 2 * QR
        q_hi = split[:, q0:q0 + QR]
        q_lo = split[:, q0 + QR:q0 + 2 * QR]
        scores = raw[:, :].rearrange("p (n t k) -> p n t k", n=2, t=QT)
        adj_hi = [split[:, i * UE:(i + 1) * UE] for i in range(NS)]
        adj_lo = [split[:, (NS + i) * UE:(NS + i + 1) * UE] for i in range(NS)]
        LE = LU * UE
        adj_in = [raw[:, 0:LE], raw[:, 2 * LE:3 * LE]]
        turned = [raw[:, LE + i * UE:LE + (i + 1) * UE] for i in range(2)] + \
                 [raw[:, 3 * LE + i * UE:3 * LE + (i + 1) * UE] for i in range(2)]
        xs = raw[:, 0:TILES * D].rearrange("p (t d) -> p t d", d=D)

        ident = sb("ident", [P, P])
        w1_sb = sb("w1_sb", [P, D])
        wl_sb, wr_sb, wh_sb, wg_sb = (yT[:, i * D:(i + 1) * D] for i in range(4))
        wT = yT[:, 4 * D:7 * D].rearrange("p (a d) -> p a d", a=3)
        dl = yT[0:TILES, 7 * D:10 * D].rearrange("p (a d) -> p a d", a=3)
        fl = yT[0:TILES, 10 * D:13 * D].rearrange("p (a d) -> p a d", a=3)
        srow = yT[0:TILES, 13 * D:14 * D]
        whg = sb("whg", [P, D])
        g_hi = sb("g_hi", [P, D], f32r)
        g_lo = sb("g_lo", [P, D], f32r)
        bias_sb = sb("bias_sb", [P, D])
        gamma_sb = sb("gamma_sb", [P, 1])
        scale = sb("scale", [P, TILES])
        stats = sb("stats", [P, TILES, 6])
        mom = sb("mom", [P, 6, TILES])
        eps_sb = sb("eps_sb", [P, 1])
        pmin = sb("pmin", [P, 2, SUNITS])
        nmax = sb("nmax", [P, 2, QT])
        rsum = sb("rsum", [P, 2, QT])
        coef = sb("coef", [P, 2, QT])
        uT = sb("uT", [P, ROWS])
        bt_half, btT = uT[:, 0:QR], uT[:, QR:2 * QR]
        hn = sb("hn", [P, CT, D])
        h2T = sb("h2T", [P, ROWS])
        zrow = hn
        outb = yT[:, 0:ROWS].rearrange("p (t d) -> p t d", t=CT)

        bank = [ctx.enter_context(nc.psum_tensor(f"bank{i}", [P, 2 * 512], f32)) for i in range(4)]
        sco_ps = [bank[0], bank[1]]
        pT_ps = [bank[2][:, 0:512], bank[2][:, 512:1024]]
        pv_ps = bank[3][:, 0:512]
        q_ps = bank[3][:, 512:512 + QR]
        one = [bank[i // 2][:, 512 * (i % 2):512 * (i % 2) + 512] for i in range(8)]
        acc_ps = [one[0], one[1]]
        row_ps, h2_ps, xw_ps = one[2], one[3], one[4]
        st_ps = [one[5], one[6]]

        x_in = sem("x_in"); resid_in = sem("resid_in"); w_in = sem("w_in")
        ident_set = sem("ident_set"); ident_ok = sem("ident_ok")
        dve_step = sem("dve_step")
        stats_ok = sem("stats_ok"); norm_ok = sem("norm_ok"); srow_ok = sem("srow_ok"); products_ok = sem("products_ok")
        key_hi_ok = sem("key_hi_ok")
        pe_setup = sem("pe_setup")
        var_ok = sem("var_ok"); std_ok = sem("std_ok")
        h_ok = sem("h_ok"); hT_ps = sem("hT_ps"); keyT_done = sem("keyT_done"); stat_done = sem("stat_done")
        q_raw = sem("q_raw"); q_split = sem("q_split"); qh_ok = sem("qh_ok")
        sco_raw = sem("sco_raw"); sco_out = sem("sco_out"); max_ok = sem("max_ok"); exp_ok = sem("exp_ok")
        pT_raw = sem("pT_raw"); pT_hi_ok = sem("pT_hi_ok"); pT_ok = sem("pT_ok"); pv_unit = sem("pv_unit")
        bt_half_ok = sem("bt_half_ok"); bt_ok = sem("bt_ok"); att_raw = sem("att_raw"); att_ok = sem("att_ok")
        adj_loaded = [sem(f"adj_loaded{i}") for i in range(NA)]
        adj_turned = sem("adj_turned"); hi_ok = sem("hi_ok"); lo_dve = sem("lo_dve"); lo_pool = sem("lo_pool")
        unit_done = sem("unit_done")
        acc_out = sem("acc_out"); rows_raw = sem("rows_raw"); rows_ok = sem("rows_ok")
        var2_ok = sem("var2_ok"); std2_ok = sem("std2_ok"); hn_ok = sem("hn_ok")
        h2_raw = sem("h2_raw"); h2T_ok = sem("h2T_ok"); xw_raw = sem("xw_raw"); xw_out = sem("xw_out")
        st_raw = sem("st_raw"); z_ok = sem("z_ok"); st_hi = sem("st_hi"); st_lo = sem("st_lo")
        out_ready = sem("out_ready"); stored = sem("stored")

        def wait(eng, s, value):
            if isinstance(value, int) and value <= 0:
                return
            eng.wait_ge(s, value)

        def chunks(eng, body, first, last, peel_end):
            body(first, 0, first // 2)
            body(first + 1, 1, first // 2)
            end = last - 2 if peel_end else last
            with eng.Fori(first // 2 + 1, end // 2) as pair:
                body(2 * pair, 0, pair)
                body(2 * pair + 1, 1, pair)
            if peel_end:
                body(last - 2, 0, last // 2 - 1)
                body(last - 1, 1, last // 2 - 1)

        def at(c, size):
            return slice(c, c + size) if isinstance(c, int) else bass.ds(c, size)

        def stacked(t2d, b):
            return t2d[:, P * b:P * (b + 1)]

        def stacked_rows(pair, odd):
            nb = ROWS // SQ
            return yT[:, :].rearrange("p (b q s) -> p q b s", q=NQ, s=SQ)[:, at(pair, 1), nb * odd:nb * (odd + 1), :]\
                .rearrange("p q b s -> p (q b) s")

        def tile_of(t3d, t):
            return t3d[:, t, :] if isinstance(t, int) else t3d[:, bass.ds(t, 1), :].rearrange("p a d -> p (a d)")

        block = ctx.enter_context(nc.Block())

        @block.sync
        def _(sp):
            xq = x.rearrange("(q b s) d -> q s b d", q=NQ, s=SQ)
            for q in range(NQ):
                sp.dma_start(xs[SQ * q:SQ * (q + 1), :, :], xq[q]).then_inc(x_in, 16)
            for t, w in ((wl_sb, w_l), (wr_sb, w_r), (wh_sb, w_h), (wg_sb, w_g), (w1_sb[:, :], weight)):
                sp.dma_start(t, w[:, :]).then_inc(w_in, 16)
            sp.dma_start(gamma_sb[:, :], gamma[None, :].to_broadcast([P, 1])).then_inc(w_in, 16)
            sp.dma_start(bias_sb[:, :], bias[None, :].to_broadcast([P, D])).then_inc(w_in, 16)
            for t, w in ((dl, d_list), (fl, filt)):
                for q in range(NQ):
                    sp.dma_start(t[:, :, SQ * q:SQ * (q + 1)],
                                 w.rearrange("j (q b s) -> q b j s", q=NQ, s=SQ)[q]).then_inc(w_in, 16)
            sp.dma_start(resid[:, :, :], x.rearrange("(t p) d -> p t d", p=P)).then_inc(resid_in, 16)

            av = adj.rearrange("(c a r) (q l w) -> q c l r a w", a=BLOCKS, r=SQ, q=NQ, l=LOADS)
            ov = out.rearrange("(c t p) d -> c p t d", t=CT, p=P)
            W = SEG // LOADS

            def load(base, c, l):
                n = base + LOADS * c + l
                s = l % NA
                if isinstance(c, int) and base == 0 and n < NA:
                    wait(sp, pT_raw, PUNITS * (QCH if n else QCH - 1))
                else:
                    wait(sp, adj_turned, LU * (n - NA + 1))
                dst = adj_in[s].rearrange("p (a w) -> p a w", a=BLOCKS)
                for q in range(NQ):
                    src = av[q, at(c, 1), l]
                    sp.dma_start(dst[SQ * q:SQ * (q + 1)], src.rearrange("c r a w -> (c r) a w"))\
                      .then_inc(adj_loaded[s], 16)

            def store(c):
                wait(sp, out_ready, c + 1)
                sp.dma_start(ov[at(c, 1)].rearrange("c p t d -> (c p) t d"), outb).then_inc(stored, 16)

            for p in range(PASSES):
                def body(c, odd, pair, p=p):
                    for l in range(LOADS):
                        load(p * CHUNKS * LOADS, c, l)
                    if p == PASSES - 1 and not (isinstance(c, int) and c == 0):
                        store(c - 1)
                chunks(sp, body, 0, CHUNKS, False)
            store(CHUNKS - 1)
            sp.wait_ge(stored, 16 * CHUNKS)

        @block.gpsimd
        def _(pool):
            nc.gpsimd.memset(eps_sb[:, :], EPS).then_inc(ident_ok, 1)
            nc.gpsimd.memset(ident[:, :], 0.0).then_inc(ident_set, 1)
            pool.wait_ge(ident_set, 1)
            nc.gpsimd.affine_select(out=ident[:, :], in_=ident[:, :], compare_op=ALU.not_equal, fill=1.0,
                                    base=0, pattern=[[-1, P]], channel_multiplier=1).then_inc(ident_ok, 1)
            for p in range(PASSES):
                def body(c, odd, pair, p=p):
                    for u in range(UNITS):
                        n = UNITS * (p * CHUNKS + c) + u
                        e = POOL_TILES[u] * ROWS
                        pool.wait_ge(hi_ok, n + 1)
                        nc.gpsimd.tensor_tensor(adj_lo[u % NS][:, 0:e], turned[u % NT][:, 0:e],
                                                adj_hi[u % NS][:, 0:e].bitcast(f32), ALU.subtract)\
                          .then_inc(lo_pool, 1)
                chunks(pool, body, 0, CHUNKS, False)

        @block.vector
        def _(dve):
            count = [0]

            def link(ins):
                count[0] = count[0] + 1
                ins.then_inc(dve_step, 1)
                dve.wait_ge(dve_step, count[0])

            def mean_and_var(t0, t1):
                m = [mom[:, i, t0:t1] for i in range(6)]
                s = stats[:, t0:t1, :]
                link(nc.vector.tensor_tensor(m[0], s[:, :, 1], s[:, :, 4], ALU.add))
                link(nc.vector.tensor_tensor(m[1], s[:, :, 1], s[:, :, 4], ALU.subtract))
                link(nc.vector.tensor_tensor(m[3], s[:, :, 2], s[:, :, 5], ALU.add))
                link(nc.vector.tensor_scalar(m[2], m[0], 0.5, None, ALU.mult))
                link(nc.vector.scalar_tensor_tensor(m[4], m[1], 0.25, m[1], ALU.mult, ALU.mult))
                return nc.vector.scalar_tensor_tensor(m[5], m[3], 1.0 / D, m[4], ALU.mult, ALU.add)

            dve.wait_ge(x_in, 16 * NQ)
            with dve.Fori(0, TILES - 3, 4) as t0:
                for t in range(4):
                    nc.vector.bn_stats(tile_of(stats, t0 + t), tile_of(xs, t0 + t)).then_inc(stats_ok, 1)
            dve.wait_ge(stats_ok, TILES)
            mean_and_var(0, TILES).then_inc(var_ok, 1)
            dve.wait_ge(std_ok, 1)
            link(nc.vector.reciprocal(mom[:, 1, :], mom[:, 0, :]))
            with dve.Fori(0, TILES - 3, 4) as t0:
                for t in range(4):
                    nc.vector.tensor_scalar(tile_of(xs, t0 + t), tile_of(xs, t0 + t), mom[:, 2, at(t0 + t, 1)],
                                            mom[:, 1, at(t0 + t, 1)], ALU.subtract, ALU.mult).then_inc(norm_ok, 1)
            dve.wait_ge(norm_ok, TILES)
            G = TILES // 4
            for g in range(4):
                h = xs[:, G * g:G * (g + 1), :]
                nc.vector.tensor_scalar(h, h, 0.0, None, ALU.max).then_inc(h_ok, 1)
            for g in range(4):
                dve.wait_ge(stat_done, g + 1)
                last = nc.vector.tensor_tensor(stat_lo[:, G * g:G * (g + 1), :], xs[:, G * g:G * (g + 1), :],
                                               stat_hi[:, G * g:G * (g + 1), :].bitcast(f32), ALU.subtract)
            link(last)

            dve.wait_ge(w_in, 16 * 15)
            link(nc.vector.tensor_tensor(fl[:, :, :], dl[:, :, :], fl[:, :, :], ALU.mult))
            link(nc.vector.tensor_tensor(fl[:, :, :], fl[:, :, :], dl[:, :, :], ALU.mult))
            link(nc.vector.tensor_tensor(srow, fl[:, 0, :], fl[:, 1, :], ALU.add))
            nc.vector.tensor_tensor(srow, srow, fl[:, 2, :], ALU.add).then_inc(srow_ok, 1)
            dve.wait_ge(pe_setup, 1)
            nc.vector.tensor_copy(wT[:, :, :], one[0][:, 0:3 * D].rearrange("p (a d) -> p a d", a=3))\
              .then_inc(products_ok, 1)
            dve.wait_ge(pe_setup, 2)
            link(nc.vector.tensor_copy(g_hi[:, :], one[1][:, 0:D]))
            link(nc.vector.tensor_tensor(g_lo[:, :], one[1][:, 0:D], g_hi[:, :].bitcast(f32), ALU.subtract))
            link(nc.vector.tensor_copy(whg[:, :], one[1][:, D:2 * D]))
            nc.vector.tensor_copy(scale[:, :], one[1][:, 2 * D:2 * D + TILES]).then_inc(products_ok, 1)

            for g in range(TILES // 4):
                dve.wait_ge(key_hi_ok, g + 1)
                hi = keyT_hi.rearrange("p (q b s) -> p b q s", q=NQ, s=SQ)[:, 4 * g:4 * g + 4]
                lo = keyT_lo.rearrange("p (q b s) -> p b q s", q=NQ, s=SQ)[:, 4 * g:4 * g + 4]
                ps = one[2 + g % 2].rearrange("p (b q s) -> p b q s", b=4, q=NQ)
                nc.vector.tensor_tensor(lo, ps, hi.bitcast(f32), ALU.subtract).then_inc(keyT_done, 1)

            dve.wait_ge(resid_in, 16)

            def q_part(c):
                wait(dve, qh_ok, c + 1)
                nc.vector.tensor_tensor(q_lo, q_ps, q_hi.bitcast(f32), ALU.subtract).then_inc(q_split, 1)

            def score_part(c, h):
                wait(dve, pT_raw, PUNITS * (c - 1))
                for u in range(SUNITS):
                    wait(dve, sco_raw, SUNITS * c + u + 1)
                    t, g = u // (N // SG), u % (N // SG)
                    dst = scores[:, h, t, :].rearrange("p (b q s) -> p q b s", q=NQ, s=SQ)[:, g]
                    nc.vector.tensor_scalar(dst, sco_ps[u % 2][:, :].rearrange("p (b s) -> p b s", s=SQ), -1.0, None,
                                            ALU.mult, ALU.min, accum_out=pmin[:, h, u:u + 1]).then_inc(sco_out, 1)
                wait(dve, sco_out, SUNITS * (c + 1))
                nc.vector.tensor_reduce(nmax[:, h, :], pmin[:, h, :].rearrange("p (t g) -> p t g", t=QT),
                                        AX.X, ALU.min).then_inc(max_ok, 1)

            def prob_part(c):
                for u in range(PUNITS):
                    n = PUNITS * c + u
                    wait(dve, pT_hi_ok, n + 1)
                    s = probT[:, u % NPT]
                    nc.vector.tensor_tensor(s[:, :, 1, :], pT_ps[u % 2].rearrange("p (k r) -> p k r", k=PK),
                                            s[:, :, 0, :].bitcast(f32), ALU.subtract).then_inc(pT_ok, 1)
                wait(dve, bt_half_ok, c + 1)
                nc.vector.tensor_tensor(btT, pv_ps[:, 0:QR], bt_half, ALU.add).then_inc(bt_ok, 1)

            def att_part(c, h, base):
                wait(dve, exp_ok, c + 1)
                count[0] = base
                link(nc.vector.reciprocal(coef[:, h, :], rsum[:, h, :]))
                link(nc.vector.tensor_scalar(coef[:, h, :], coef[:, h, :], gamma_sb[:, 0:1], None, ALU.mult))
                wait(dve, att_raw, c + 1)
                for t in range(QT):
                    r = tile_of(resid, QT * c + t)
                    last = nc.vector.scalar_tensor_tensor(r, pv_ps[:, D * t:D * (t + 1)], coef[:, h, t:t + 1], r,
                                                          ALU.mult, ALU.add)
                last.then_inc(att_ok, 1)

            base0 = count[0]
            q_part(0)
            score_part(0, 0)
            q_part(1)
            score_part(1, 1)
            q_part(2)
            prob_part(0)

            def step(c, h):
                score_part(c + 1, 1 - h)
                att_part(c - 1, 1 - h, base0 + 2 * (c - 1))
                q_part(c + 2)
                prob_part(c)
            with dve.Fori(1, QCH - 4, 2) as c:
                step(c, 1)
                step(c + 1, 0)
            c = QCH - 3
            step(c, 1)
            score_part(c + 2, 1)
            att_part(c, 1, base0 + 2 * c)
            prob_part(c + 1)
            att_part(c + 1, 0, base0 + 2 * (c + 1))
            prob_part(c + 2)
            att_part(c + 2, 1, base0 + 2 * (c + 2))
            dve.wait_ge(att_ok, QCH)

            def turn(c, u, p):
                n = UNITS * (p * CHUNKS + c) + u
                l = u // LU
                if u % LU == 0:
                    m = LOADS * (p * CHUNKS + c) + l
                    wait(dve, adj_loaded[l % NA], LOAD_INC * ((LOADS // NA) * (p * CHUNKS + c) + l // NA + 1))
                wait(dve, hi_ok, n - NT + 1)
                wait(dve, lo_pool, n - NT + 1)
                src = adj_in[l % NA].rearrange("p (a b s) -> p b a s", a=BLOCKS, s=SQ)[:, UT * (u % LU):UT * (u % LU) + UT]
                dst = turned[u % NT].rearrange("p (b a s) -> p b a s", b=UT, s=SQ)
                nc.vector.transpose(dst, src).then_inc(adj_turned, 1)

            def low(c, u, p):
                n = UNITS * (p * CHUNKS + c) + u
                e = POOL_TILES[u] * ROWS
                wait(dve, hi_ok, n + 1)
                nc.vector.tensor_tensor(adj_lo[u % NS][:, e:], turned[u % NT][:, e:],
                                        adj_hi[u % NS][:, e:].bitcast(f32), ALU.subtract).then_inc(lo_dve, 1)

            LN_LINKS = 1 + 5 + 1

            def rows_first(c, base):
                count[0] = base
                wait(dve, rows_raw, c + 1)
                r = resid[:, at(CT * c, CT), :]
                wait(dve, h2_raw, c)
                nc.vector.tensor_tensor(hn[:, :, :], row_ps.rearrange("p (t d) -> p t d", t=CT), r, ALU.add)\
                  .then_inc(rows_ok, 1)
                dve.wait_ge(rows_ok, c + 1)
                for t in range(CT):
                    nc.vector.bn_stats(stats[:, t, :], hn[:, t, :])
                link(nc.vector.tensor_copy(r, hn[:, :, :]))
                mean_and_var(0, CT).then_inc(var2_ok, 1)

            def rows_second(c, base):
                count[0] = base + 6
                wait(dve, std2_ok, c + 1)
                link(nc.vector.reciprocal(mom[:, 1, 0:CT], mom[:, 0, 0:CT]))
                for t in range(CT):
                    last = nc.vector.tensor_scalar(hn[:, t, :], hn[:, t, :], mom[:, 2, t:t + 1], mom[:, 1, t:t + 1],
                                                   ALU.subtract, ALU.mult)
                last.then_inc(hn_ok, 1)

            def rows_out(c, base):
                count[0] = base
                wait(dve, rows_raw, CHUNKS + c + 1)
                wait(dve, stored, 16 * c)
                r = resid[:, at(CT * c, CT), :]
                o = outb
                link(nc.vector.tensor_tensor(o, row_ps.rearrange("p (t d) -> p t d", t=CT), r, ALU.add))
                for t in range(CT):
                    last = nc.vector.tensor_tensor(o[:, t, :], o[:, t, :], bias_sb[:, :], ALU.add)
                last.then_inc(out_ready, 1)

            turn(0, 0, 0)
            for p in range(PASSES):
                base_p = count[0]

                def body(c, odd, pair, p=p, base_p=base_p):
                    first = isinstance(c, int) and c == 0
                    end = isinstance(c, int) and c == CHUNKS - 1 and p == PASSES - 1
                    for u in range(UNITS):
                        if u < UNITS - 1:
                            turn(c, u + 1, p)
                        elif not end:
                            turn(c + 1, 0, p)
                        low(c, u, p)
                        if not first and p == 0 and u == 1:
                            rows_first(c - 1, base_p + LN_LINKS * (c - 1))
                        if not first and p == 0 and u == 3:
                            rows_second(c - 1, base_p + LN_LINKS * (c - 1))
                        if not first and p == 2 and u == 2:
                            rows_out(c - 1, base_p + (c - 1))
                chunks(dve, body, 0, CHUNKS, p == PASSES - 1)
                if p == 0:
                    rows_first(CHUNKS - 1, base_p + LN_LINKS * (CHUNKS - 1))
                    rows_second(CHUNKS - 1, base_p + LN_LINKS * (CHUNKS - 1))
                if p == 2:
                    rows_out(CHUNKS - 1, base_p + CHUNKS - 1)
                if p < PASSES - 1:
                    for g in range(TILES // 4):
                        m = p * (TILES // 4) + g
                        ps = st_ps[g % 2].rearrange("p (t d) -> p t d", t=4)
                        hi, lo = stat_hi[:, 4 * g:4 * g + 4, :], stat_lo[:, 4 * g:4 * g + 4, :]
                        if p == 0:
                            dve.wait_ge(st_hi, m + 1)
                            nc.vector.tensor_tensor(lo, ps, hi.bitcast(f32), ALU.subtract).then_inc(st_lo, 1)
                        else:
                            dve.wait_ge(st_raw, m + 1)
                            if g > 0:
                                dve.wait_ge(st_lo, m)
                            for t in range(4):
                                last = nc.vector.tensor_scalar(zrow[:, t, :], ps[:, t, :],
                                                               scale[:, 4 * g + t:4 * g + t + 1], None, ALU.mult)
                            last.then_inc(z_ok, 1)
                            dve.wait_ge(st_hi, m + 1)
                            nc.vector.tensor_tensor(lo, zrow[:, :, :], hi.bitcast(f32), ALU.subtract)\
                              .then_inc(st_lo, 1)

        @block.scalar
        def _(act):
            act.wait_ge(ident_ok, 2)
            act.wait_ge(var_ok, 1)
            nc.scalar.activation(mom[:, 0, :], mom[:, 5, :], ACT.Sqrt, bias=eps_sb[:, 0:1]).then_inc(std_ok, 1)
            G = TILES // 4
            for g in range(4):
                act.wait_ge(h_ok, g + 1)
                nc.scalar.activation(stat_hi[:, G * g:G * (g + 1), :], xs[:, G * g:G * (g + 1), :],
                                     ACT.Copy).then_inc(stat_done, 1)
            for g in range(TILES // 4):
                act.wait_ge(hT_ps, g + 1)
                hi = keyT_hi.rearrange("p (q b s) -> p b q s", q=NQ, s=SQ)[:, 4 * g:4 * g + 4]
                ps = one[2 + g % 2].rearrange("p (b q s) -> p b q s", b=4, q=NQ)
                nc.scalar.activation(hi, ps, ACT.Copy).then_inc(key_hi_ok, 1)

            def q_part(c):
                wait(act, q_raw, c + 1)
                wait(act, sco_raw, SUNITS * c)
                nc.scalar.activation(q_hi, q_ps, ACT.Copy).then_inc(qh_ok, 1)

            def exp_part(c, h):
                wait(act, max_ok, c + 1)
                for t in range(QT):
                    last = nc.scalar.activation(scores[:, h, t, :], scores[:, h, t, :], ACT.Exp,
                                                bias=nmax[:, h, t:t + 1], scale=-1.0, accum_out=rsum[:, h, t:t + 1])
                last.then_inc(exp_ok, 1)

            def prob_part(c):
                for u in range(PUNITS):
                    n = PUNITS * c + u
                    wait(act, pT_raw, n + 1)
                    wait(act, pv_unit, n - NPT + 1)
                    nc.scalar.activation(probT[:, u % NPT][:, :, 0, :],
                                         pT_ps[u % 2].rearrange("p (k r) -> p k r", k=PK), ACT.Copy)\
                      .then_inc(pT_hi_ok, 1)
                wait(act, pv_unit, PUNITS * (c + 1))
                nc.scalar.activation(bt_half, pv_ps[:, QR:2 * QR], ACT.Copy).then_inc(bt_half_ok, 1)

            q_part(0)
            q_part(1)
            exp_part(0, 0)

            def step(c, h):
                q_part(c + 2)
                prob_part(c)
                exp_part(c + 1, 1 - h)
            step(0, 0)
            with act.Fori(1, QCH - 4, 2) as c:
                step(c, 1)
                step(c + 1, 0)
            step(QCH - 3, 1)
            prob_part(QCH - 2)
            exp_part(QCH - 1, 1)
            prob_part(QCH - 1)

            def take(c, h, p, pair):
                wait(act, unit_done, UNITS * (p * CHUNKS + c + 1))
                if p == 1:
                    dst = stacked_rows(pair, h)
                else:
                    dst = uT[:, :]
                    wait(act, rows_raw, (p // 2) * CHUNKS + c)
                src = acc_ps[h].rearrange("p (b s) -> p b s", s=SQ) if p == 1 else acc_ps[h]
                nc.scalar.activation(dst, src, ACT.Copy).then_inc(acc_out, 1)

            def std2(c):
                wait(act, var2_ok, c + 1)
                nc.scalar.activation(mom[:, 0, 0:CT], mom[:, 5, 0:CT], ACT.Sqrt, bias=eps_sb[:, 0:1]).then_inc(std2_ok, 1)

            def relu_out(c):
                wait(act, h2_raw, c + 1)
                wait(act, xw_raw, c)
                nc.scalar.activation(h2T[:, :], h2_ps, ACT.Relu).then_inc(h2T_ok, 1)

            def xw_part(c, h, pair):
                wait(act, xw_raw, c + 1)
                nc.scalar.activation(stacked_rows(pair, h), xw_ps.rearrange("p (b s) -> p b s", s=SQ), ACT.Copy).then_inc(xw_out, 1)

            for p in range(PASSES):
                def body(c, odd, pair, p=p):
                    first = isinstance(c, int) and c == 0
                    h = 1 - odd
                    for u in range(UNITS):
                        n = UNITS * (p * CHUNKS + c) + u
                        wait(act, adj_turned, n + 1)
                        wait(act, unit_done, n - NS + 1)
                        nc.scalar.activation(adj_hi[u % NS], turned[u % NT], ACT.Copy).then_inc(hi_ok, 1)
                        if first:
                            continue
                        if u == 0:
                            take(c - 1, h, p, pair if odd else pair - 1)
                        if p == 0 and u == 2:
                            std2(c - 1)
                        if p == 0 and u == 5:
                            relu_out(c - 1)
                        if p == 0 and u == 7:
                            xw_part(c - 1, h, pair if odd else pair - 1)
                chunks(act, body, 0, CHUNKS, False)
                take(CHUNKS - 1, 1, p, CHUNKS // 2 - 1)
                if p == 0:
                    std2(CHUNKS - 1)
                    relu_out(CHUNKS - 1)
                    xw_part(CHUNKS - 1, 1, CHUNKS // 2 - 1)
                if p < PASSES - 1:
                    for g in range(TILES // 4):
                        m = p * (TILES // 4) + g
                        hi = stat_hi[:, 4 * g:4 * g + 4, :]
                        if p == 0:
                            act.wait_ge(st_raw, m + 1)
                            src = st_ps[g % 2].rearrange("p (t d) -> p t d", t=4)
                        else:
                            act.wait_ge(z_ok, g + 1)
                            src = zrow[:, :, :]
                        nc.scalar.activation(hi, src, ACT.Copy).then_inc(st_hi, 1)

        @block.tensor
        def _(pe):
            mm, tr = nc.tensor.matmul, nc.tensor.transpose
            pe.wait_ge(ident_ok, 2)
            pe.wait_ge(w_in, 16 * 15)
            for i, w in enumerate((wl_sb, wr_sb, wh_sb)):
                last = tr(one[0][:, D * i:D * (i + 1)], w, ident[:, :])
            last.then_inc(pe_setup, 1)
            for g in range(TILES // 4):
                pe.wait_ge(h_ok, g // 2 + 1)
                wait(pe, keyT_done, g - 1)
                for b in range(4):
                    last = tr(one[2 + g % 2][:, P * b:P * (b + 1)], xs[:, 4 * g + b, :], ident[:, :])
                last.then_inc(hT_ps, 1)
                if g == 1:
                    pe.wait_ge(products_ok, 1)
                    pe.wait_ge(srow_ok, 1)
                    mm(one[1][:, 0:D], wT[:, 0, :], wT[:, 1, :], start=True, stop=True)
                    mm(one[1][:, D:2 * D], wT[:, 2, :], wg_sb, start=True, stop=True)
                    tr(one[1][:, 2 * D:2 * D + TILES], srow, ident[0:TILES, 0:TILES]).then_inc(pe_setup, 1)

            def queries(c):
                wait(pe, q_split, c)
                k_hi, k_lo = keyT_hi[:, at(QR * c, QR)], keyT_lo[:, at(QR * c, QR)]
                mm(q_ps, g_hi[:, :], k_hi, start=True, stop=False)
                mm(q_ps, g_hi[:, :], k_lo, start=False, stop=False)
                mm(q_ps, g_lo[:, :], k_hi, start=False, stop=True).then_inc(q_raw, 1)

            def score_part(c):
                wait(pe, q_split, c + 1)
                for u in range(SUNITS):
                    wait(pe, sco_out, SUNITS * c + u - 1)
                    t, g = u // (N // SG), u % (N // SG)
                    for a, k, s, e in ((q_hi, keyT_hi, True, False), (q_hi, keyT_lo, False, False),
                                       (q_lo, keyT_hi, False, True)):
                        for j in range(2):
                            col = SG * g + 512 * j
                            last = mm(sco_ps[u % 2][:, 512 * j:512 * (j + 1)], a[:, P * t:P * (t + 1)],
                                      k[:, col:col + 512], start=s, stop=e)
                    last.then_inc(sco_raw, 1)

            def prob_turn(c, h, u):
                n = PUNITS * c + u
                wait(pe, pT_ok, n - 1)
                for k in range(PK):
                    for t in range(QT):
                        last = tr(pT_ps[u % 2][:, QR * k + P * t:QR * k + P * (t + 1)],
                                  stacked(scores[:, h, t, :], PK * u + k), ident[:, :])
                last.then_inc(pT_raw, 1)

            def prob_use(c, u):
                wait(pe, pT_ok, PUNITS * c + u + 1)
                for k in range(PK):
                    b = PK * u + k
                    s = probT[:, u % NPT, k]
                    both = s.rearrange("p h r -> p (h r)")
                    if b == 0:
                        mm(pv_ps, stat_hi[:, b, :], both, start=True, stop=False)
                        last = mm(pv_ps[:, 0:QR], stat_lo[:, b, :], s[:, 0, :], start=False, stop=False)
                    else:
                        mm(pv_ps[:, 0:QR], stat_lo[:, b, :], s[:, 0, :], start=False, stop=False)
                        last = mm(pv_ps, stat_hi[:, b, :], both, start=False, stop=b == TILES - 1)
                last.then_inc(pv_unit, 1)

            def prob_part(c, h):
                wait(pe, exp_ok, c + 1)
                prob_turn(c, h, 0)
                prob_turn(c, h, 1)
                wait(pe, att_ok, c)
                for u in range(PUNITS):
                    prob_use(c, u)
                    if u + 2 < PUNITS:
                        prob_turn(c, h, u + 2)

            def att_rows(c):
                wait(pe, bt_ok, c + 1)
                for t in range(QT):
                    last = mm(pv_ps[:, D * t:D * (t + 1)], btT[:, P * t:P * (t + 1)], whg[:, :], start=True, stop=True)
                last.then_inc(att_raw, 1)

            pe.wait_ge(products_ok, 2)
            pe.wait_ge(keyT_done, TILES // 4)
            queries(0)
            score_part(0)
            queries(1)
            score_part(1)
            queries(2)
            prob_part(0, 0)

            def step(c, h):
                score_part(c + 1)
                att_rows(c - 1)
                queries(c + 2)
                prob_part(c, h)
            with pe.Fori(1, QCH - 4, 2) as c:
                step(c, 1)
                step(c + 1, 0)
            c = QCH - 3
            step(c, 1)
            score_part(c + 2)
            att_rows(c)
            prob_part(c + 1, 0)
            att_rows(c + 1)
            prob_part(c + 2, 1)
            att_rows(c + 2)

            def unit(c, u, a, p):
                n = UNITS * (p * CHUNKS + c) + u
                wait(pe, lo_pool, n + 1)
                wait(pe, lo_dve, n + 1)
                for b in range(UT):
                    k = UT * u + b
                    hi, lo = adj_hi[u % NS][:, ROWS * b:ROWS * (b + 1)], adj_lo[u % NS][:, ROWS * b:ROWS * (b + 1)]
                    mm(a, stat_hi[:, k, :], hi, start=k == 0, stop=False)
                    mm(a, stat_hi[:, k, :], lo, start=False, stop=False)
                    last = mm(a, stat_lo[:, k, :], hi, start=False, stop=k == TILES - 1)
                last.then_inc(unit_done, 1)

            def sum_rows(c, p):
                wait(pe, acc_out, p * CHUNKS + c + 1)
                if p == 0:
                    wait(pe, rows_ok, c)
                else:
                    wait(pe, out_ready, c)
                for t in range(CT):
                    last = tr(row_ps[:, P * t:P * (t + 1)], uT[:, P * t:P * (t + 1)], ident[:, :])
                last.then_inc(rows_raw, 1)

            def norm_cols(c):
                wait(pe, hn_ok, c + 1)
                wait(pe, h2T_ok, c)
                for t in range(CT):
                    last = tr(h2_ps[:, P * t:P * (t + 1)], hn[:, t, :], ident[:, :])
                last.then_inc(h2_raw, 1)

            def times_weight(c):
                wait(pe, h2T_ok, c + 1)
                wait(pe, xw_out, c)
                mm(xw_ps, w1_sb[:, :], h2T[:, :], start=True, stop=True).then_inc(xw_raw, 1)

            for p in range(PASSES):
                def body(c, odd, pair, p=p):
                    first = isinstance(c, int) and c == 0
                    h = odd
                    wait(pe, acc_out, p * CHUNKS + c - 1)
                    for u in range(UNITS):
                        unit(c, u, acc_ps[h], p)
                        if first:
                            continue
                        if p != 1 and u == 1:
                            sum_rows(c - 1, p)
                        if p == 0 and u == 5:
                            norm_cols(c - 1)
                        if p == 0 and u == 6:
                            times_weight(c - 1)
                chunks(pe, body, 0, CHUNKS, False)
                if p != 1:
                    sum_rows(CHUNKS - 1, p)
                if p == 0:
                    norm_cols(CHUNKS - 1)
                    times_weight(CHUNKS - 1)
                    pe.wait_ge(xw_out, CHUNKS)
                if p == 1:
                    pe.wait_ge(acc_out, 2 * CHUNKS)
                if p < PASSES - 1:
                    for g in range(TILES // 4):
                        m = p * (TILES // 4) + g
                        if g >= 2:
                            pe.wait_ge(st_lo, m - 1)
                        for t in range(4):
                            last = tr(st_ps[g % 2][:, P * t:P * (t + 1)], stacked(yT[:, :], 4 * g + t), ident[:, :])
                        last.then_inc(st_raw, 1)
                    pe.wait_ge(st_lo, (p + 1) * (TILES // 4))


_INS = ['x', 'adj', 'L0_gnn_W_l', 'L0_gnn_W_r', 'L0_gnn_W_h', 'L0_gnn_W_g', 'L0_gnn_gamma', 'L1_gnn_d_list',
        'L1_gnn_weight', 'L1_gnn_filt', 'L1_gnn_bias']
_OUTS = [((4096, 128), 'float32')]


def kernel(**inputs):
    import numpy as _np
    import concourse.bacc as _bacc
    from concourse import mybir as _mybir
    from concourse.bass_utils import run_bass_kernel_spmd as _run

    nc = _bacc.Bacc("TRN2", target_bir_lowering=False, num_devices=1)
    arrays, args = {}, []
    for name in _INS:
        a = _np.ascontiguousarray(inputs[name])
        arrays[f"in_{name}_dram"] = a
        args.append(nc.dram_tensor(f"in_{name}_dram", a.shape, _mybir.dt.from_np(a.dtype), kind="ExternalInput").ap())
    for i, (shape, dtype) in enumerate(_OUTS):
        dt = _mybir.dt.from_np(_np.dtype(dtype))
        args.append(nc.dram_tensor(f"out_{i}_dram", shape, dt, kind="ExternalOutput").ap())
    preln_attention_graph_kernel(nc, *args)
    r = _run(nc, [arrays], core_ids=[0])
    return r.results[0]["out_0_dram"]
```

```python
import concourse.bass as bass
from concourse import mybir
from contextlib import ExitStack


def preln_attention_graph_kernel(nc, x, adj, w_l, w_r, w_h, w_g, gamma, d_list, weight, filt, bias, out):
    f32, f32r = mybir.dt.float32, mybir.dt.float32r
    ALU, ACT, AX = mybir.AluOpType, mybir.ActivationFunctionType, mybir.AxisListType

    N, D = x.shape
    P = 128
    SQ = 32
    NQ = P // SQ
    TILES = N // P
    HALF = N // 2
    SEG = HALF // NQ
    HT = TILES // 2
    EPS = 1e-5

    ROWS = 512
    BLOCKS = ROWS // SQ
    CT = ROWS // P
    GC = HALF // ROWS
    UT = 2
    UNITS = HT // UT
    UE = UT * ROWS
    LU = 4
    LOADS = UNITS // LU
    NT, NH, NL = 4, 8, 4
    LOAD_INC = 16 * NQ
    POOL_E = 704
    RT = 4
    RG = HT // RT
    GROUPS = ((0, (0, 1), False),
              (1, (1, 0), True),
              (1, (1,), False),
              (0, (0, 1), True),
              (1, (1, 0), False),
              (0, (0,), False))
    FIRST_VISIT = [GC * sum(len(x[1]) for x in GROUPS[:g]) for g in range(len(GROUPS))]

    QR = 256
    QCH = N // QR
    QT = QR // P
    SG = 1024
    SUNITS = QT * (N // SG)
    PK = 2
    PUNITS = TILES // PK
    NPT = 4

    ctx = ExitStack()
    with ctx:
        def sb(name, shape, dt=f32):
            return ctx.enter_context(nc.sbuf_tensor(name, shape, dt))

        def sem(name):
            return ctx.enter_context(nc.semaphore(name))

        stat_hi = sb("stat_hi", [P, TILES, D], f32r)
        stat_lo = sb("stat_lo", [P, TILES, D], f32r)
        keys = sb("keys", [P, 2 * N], f32r)
        resid = sb("resid", [P, TILES, D])
        split = sb("split", [P, (NH + NL) * UE], f32r)
        raw = sb("raw", [P, 2 * QT * N])
        keyT_hi, keyT_lo = keys[:, 0:N], keys[:, N:2 * N]
        probT = split[:, 0:NPT * PK * 2 * QR].rearrange("p (n k h r) -> p n k h r", n=NPT, k=PK, h=2)
        q0 = NPT * PK * 2 * QR
        q_hi = split[:, q0:q0 + QR]
        q_lo = split[:, q0 + QR:q0 + 2 * QR]
        scores = raw[:, :].rearrange("p (n t k) -> p n t k", n=2, t=QT)
        xw_hi = keyT_hi.rearrange("p (t d) -> p t d", d=D)
        xw_lo = keyT_lo.rearrange("p (t d) -> p t d", d=D)
        adj_hi = [split[:, i * UE:(i + 1) * UE] for i in range(NH)]
        adj_lo = [split[:, (NH + i) * UE:(NH + i + 1) * UE] for i in range(NL)]
        LE = LU * UE
        adj_in = [raw[:, 0:LE], raw[:, 2 * LE:3 * LE]]
        turned = [raw[:, LE + i * UE:LE + (i + 1) * UE] for i in range(NT)]
        xwT = raw[:, 3 * LE:3 * LE + HALF]
        yT = raw[:, 3 * LE + HALF:3 * LE + 2 * HALF]
        xs = raw[:, 0:TILES * D].rearrange("p (t d) -> p t d", d=D)
        w0 = TILES * D
        wl_sb, wr_sb, wh_sb, wg_sb = (raw[:, w0 + i * D:w0 + (i + 1) * D] for i in range(4))
        wT = raw[:, w0 + 4 * D:w0 + 7 * D].rearrange("p (a d) -> p a d", a=3)
        dl = raw[0:TILES, w0 + 7 * D:w0 + 10 * D].rearrange("p (a d) -> p a d", a=3)
        fl = raw[0:TILES, w0 + 10 * D:w0 + 13 * D].rearrange("p (a d) -> p a d", a=3)
        srow = raw[0:TILES, w0 + 13 * D:w0 + 14 * D]

        ident = sb("ident", [P, P])
        w1_sb = sb("w1_sb", [P, D])
        whg = sb("whg", [P, D])
        g_hi = sb("g_hi", [P, D], f32r)
        g_lo = sb("g_lo", [P, D], f32r)
        bias_sb = sb("bias_sb", [P, CT, D])
        gamma_sb = sb("gamma_sb", [P, 1])
        scale = sb("scale", [P, TILES])
        stats = sb("stats", [P, TILES, 6])
        mom = sb("mom", [P, 6, TILES])
        eps_sb = sb("eps_sb", [P, 1])
        pmin = sb("pmin", [P, 2, SUNITS])
        nmax = sb("nmax", [P, 2, QT])
        rsum = sb("rsum", [P, 2, QT])
        coef = sb("coef", [P, 2, QT])
        uT = sb("uT", [P, ROWS])
        bt_half, btT = uT[:, 0:QR], uT[:, QR:2 * QR]
        hn = sb("hn", [P, CT, D])
        zrow = hn
        h2T = sb("h2T", [P, ROWS])
        outb = sb("outb", [P, CT, D])

        bank = [ctx.enter_context(nc.psum_tensor(f"bank{i}", [P, 2 * 512], f32)) for i in range(4)]
        sco_ps = [bank[0], bank[1]]
        pT_ps = [bank[2][:, 0:512], bank[2][:, 512:1024], bank[3][:, 512:1024]]
        pv_ps = bank[3][:, 0:512]
        q_ps = bank[3][:, 512:512 + QR]
        one = [bank[i // 2][:, 512 * (i % 2):512 * (i % 2) + 512] for i in range(8)]
        acc_ps, dual_ps = bank[0], bank[1]
        row_ps, h2_ps, xw_ps = one[4], one[5], one[6]
        st_ps = [one[7], one[6]]

        x_in = sem("x_in"); resid_in = sem("resid_in"); w_in = sem("w_in")
        ident_set = sem("ident_set"); ident_ok = sem("ident_ok")
        dve_step = sem("dve_step")
        stats_ok = sem("stats_ok"); norm_ok = sem("norm_ok"); srow_ok = sem("srow_ok"); products_ok = sem("products_ok")
        key_hi_ok = sem("key_hi_ok")
        pe_setup = sem("pe_setup")
        var_ok = sem("var_ok"); std_ok = sem("std_ok")
        h_ok = sem("h_ok"); hT_ps = sem("hT_ps"); keyT_done = sem("keyT_done"); stat_done = sem("stat_done")
        q_raw = sem("q_raw"); q_split = sem("q_split"); qh_ok = sem("qh_ok")
        sco_raw = sem("sco_raw"); sco_out = sem("sco_out"); max_ok = sem("max_ok"); exp_ok = sem("exp_ok")
        pT_raw = sem("pT_raw"); pT_hi_ok = sem("pT_hi_ok"); pT_ok = sem("pT_ok"); pv_unit = sem("pv_unit")
        bt_half_ok = sem("bt_half_ok"); bt_ok = sem("bt_ok"); att_raw = sem("att_raw"); att_ok = sem("att_ok")
        adj_loaded = [sem(f"adj_loaded{i}") for i in range(LOADS)]
        adj_turned = sem("adj_turned"); hi_ok = sem("hi_ok"); lo_dve = sem("lo_dve"); lo_pool = sem("lo_pool")
        unit_done = sem("unit_done")
        acc_out = sem("acc_out"); dual_out = sem("dual_out"); rows_raw = sem("rows_raw"); rows_ok = sem("rows_ok")
        var2_ok = sem("var2_ok"); std2_ok = sem("std2_ok"); hn_ok = sem("hn_ok")
        h2_raw = sem("h2_raw"); h2T_ok = sem("h2T_ok"); xw_raw = sem("xw_raw"); xw_out = sem("xw_out")
        y_ok = sem("y_ok"); part_raw = sem("part_raw"); part_ok = sem("part_ok")
        st_raw = sem("st_raw"); z_ok = sem("z_ok"); st_hi = sem("st_hi"); st_lo = sem("st_lo")
        out_ready = sem("out_ready"); stored = sem("stored")

        from_one = {"scalar": (acc_out, dual_out, h2T_ok, xw_out), "vector": (rows_ok, y_ok, part_ok, out_ready),
                    "tensor": (rows_raw, h2_raw, part_raw, xw_raw), "sync": (stored,)}

        def start_counts(eng, name):
            for s in from_one[name]:
                eng.sem_inc(s, 1)

        def wait(eng, s, value):
            if isinstance(value, int) and value <= 0:
                return
            eng.wait_ge(s, value + 1 if any(s is x for xs_ in from_one.values() for x in xs_) else value)

        def passes(eng, chunk, flush):
            last = None
            for g in range(len(GROUPS)):
                chunk(g, 0, last)
                with eng.Fori(1, GC) as k:
                    chunk(g, k, (g, k - 1))
                last = (g, GC - 1)
            flush(last)

        def visit_number(g, k, j):
            return FIRST_VISIT[g] + len(GROUPS[g][1]) * k + j

        def ahead(before, plan, u):
            for pos, step in plan:
                if pos == u:
                    step()

        def at(c, size):
            return slice(c, c + size) if isinstance(c, int) else bass.ds(c, size)

        def stacked(t2d, b):
            return t2d[:, P * b:P * (b + 1)]

        def key_columns(kT, g):
            v = kT.rearrange("p (h q b s) -> p h b q s", h=2, q=NQ, s=SQ)
            return v[:, g // (HT // 4), 4 * (g % (HT // 4)):4 * (g % (HT // 4)) + 4]

        def stacked_rows(yh, q):
            return yh.rearrange("p (b q s) -> p q b s", q=NQ, s=SQ)[:, at(q, 1)].rearrange("p q b s -> p (q b) s")

        def tile_of(t3d, t):
            return t3d[:, t, :] if isinstance(t, int) else t3d[:, bass.ds(t, 1), :].rearrange("p a d -> p (a d)")

        W_LOADS = 5 + 1 + CT + 2 * 2 * NQ

        block = ctx.enter_context(nc.Block())

        @block.sync
        def _(sp):
            start_counts(sp, "sync")
            xq = x.rearrange("(h q b s) d -> h q s b d", h=2, q=NQ, s=SQ)
            for h in range(2):
                for q in range(NQ):
                    sp.dma_start(xs[SQ * q:SQ * (q + 1), HT * h:HT * (h + 1), :], xq[h, q]).then_inc(x_in, 16)
            for t, w in ((wl_sb, w_l), (wr_sb, w_r), (wh_sb, w_h), (wg_sb, w_g), (w1_sb[:, :], weight)):
                sp.dma_start(t, w[:, :]).then_inc(w_in, 16)
            sp.dma_start(gamma_sb[:, :], gamma[None, :].to_broadcast([P, 1])).then_inc(w_in, 16)
            for t in range(CT):
                sp.dma_start(bias_sb[:, t, :], bias[None, :].to_broadcast([P, D])).then_inc(w_in, 16)
            for t, w in ((dl, d_list), (fl, filt)):
                for h in range(2):
                    for q in range(NQ):
                        sp.dma_start(t[HT * h:HT * (h + 1), :, SQ * q:SQ * (q + 1)],
                                     w.rearrange("j (h q b s) -> h q b j s", h=2, q=NQ, s=SQ)[h, q]).then_inc(w_in, 16)
            sp.dma_start(resid[:, :, :], x.rearrange("(t p) d -> p t d", p=P)).then_inc(resid_in, 16)

            av = adj.rearrange("(c a r) (h q l w) -> q h c l r a w", a=BLOCKS, r=SQ, h=2, q=NQ, l=LOADS)
            ov = out.rearrange("(c t p) d -> c p t d", t=CT, p=P)

            def load(g, k, j, l, rows):
                cols = GROUPS[g][1]
                v = visit_number(g, k, j)
                if isinstance(v, int) and v == 0:
                    sp.wait_ge(pT_raw, PUNITS * (QCH - 1 + l))
                else:
                    wait(sp, adj_turned, UNITS * v + LU * l - (LOADS - 1) * LU)
                dst = adj_in[l].rearrange("p (a w) -> p a w", a=BLOCKS)
                for q in reversed(range(NQ)):
                    src = av[q, cols[j], at(rows, 1), l]
                    sp.dma_start(dst[SQ * q:SQ * (q + 1)], src.rearrange("c r a w -> (c r) a w"))\
                      .then_inc(adj_loaded[l], 16)

            def store(g, k):
                n = GC * (g - 4) + k
                wait(sp, out_ready, n + 1)
                sp.dma_start(ov[at(GC * GROUPS[g][0] + k, 1)].rearrange("c p t d -> (c p) t d"), outb[:, :, :])\
                  .then_inc(stored, 16)

            def chunk(g, k, after):
                rows = GC * GROUPS[g][0] + k
                if not isinstance(k, int):
                    rows = sp.snap(rows)
                for j in range(len(GROUPS[g][1])):
                    for l in range(LOADS):
                        load(g, k, j, l, rows)
                if after and after[0] >= 4:
                    store(*after)
            passes(sp, chunk, lambda after: store(*after))
            wait(sp, stored, 16 * 2 * GC)

        @block.gpsimd
        def _(pool):
            nc.gpsimd.memset(eps_sb[:, :], EPS).then_inc(ident_ok, 1)
            nc.gpsimd.memset(ident[:, :], 0.0).then_inc(ident_set, 1)
            pool.wait_ge(ident_set, 1)
            nc.gpsimd.affine_select(out=ident[:, :], in_=ident[:, :], compare_op=ALU.not_equal, fill=1.0,
                                    base=0, pattern=[[-1, P]], channel_multiplier=1).then_inc(ident_ok, 1)

            def chunk(g, k, after):
                for j in range(len(GROUPS[g][1])):
                    for u in range(UNITS):
                        n = UNITS * visit_number(g, k, j) + u
                        wait(pool, hi_ok, n + 1)
                        wait(pool, unit_done, n - NL + 1)
                        nc.gpsimd.tensor_tensor(adj_lo[u % NL][:, 0:POOL_E], turned[u % NT][:, 0:POOL_E],
                                                adj_hi[u % NH][:, 0:POOL_E].bitcast(f32), ALU.subtract)\
                          .then_inc(lo_pool, 1)
            passes(pool, chunk, lambda after: None)

        @block.vector
        def _(dve):
            start_counts(dve, "vector")
            count = [0]

            def link(ins):
                count[0] = count[0] + 1
                ins.then_inc(dve_step, 1)
                dve.wait_ge(dve_step, count[0])

            def mean_and_var(t0, t1):
                m = [mom[:, i, t0:t1] for i in range(6)]
                s = stats[:, t0:t1, :]
                link(nc.vector.tensor_tensor(m[0], s[:, :, 1], s[:, :, 4], ALU.add))
                link(nc.vector.tensor_tensor(m[1], s[:, :, 1], s[:, :, 4], ALU.subtract))
                link(nc.vector.tensor_tensor(m[3], s[:, :, 2], s[:, :, 5], ALU.add))
                link(nc.vector.tensor_scalar(m[2], m[0], 0.5, None, ALU.mult))
                link(nc.vector.scalar_tensor_tensor(m[4], m[1], 0.25, m[1], ALU.mult, ALU.mult))
                return nc.vector.scalar_tensor_tensor(m[5], m[3], 1.0 / D, m[4], ALU.mult, ALU.add)

            dve.wait_ge(x_in, 16 * 2 * NQ)
            with dve.Fori(0, TILES - 3, 4) as t0:
                for t in range(4):
                    nc.vector.bn_stats(tile_of(stats, t0 + t), tile_of(xs, t0 + t)).then_inc(stats_ok, 1)
            dve.wait_ge(stats_ok, TILES)
            mean_and_var(0, TILES).then_inc(var_ok, 1)
            dve.wait_ge(std_ok, 1)
            link(nc.vector.reciprocal(mom[:, 1, :], mom[:, 0, :]))
            with dve.Fori(0, TILES - 3, 4) as t0:
                for t in range(4):
                    nc.vector.tensor_scalar(tile_of(xs, t0 + t), tile_of(xs, t0 + t), mom[:, 2, at(t0 + t, 1)],
                                            mom[:, 1, at(t0 + t, 1)], ALU.subtract, ALU.mult).then_inc(norm_ok, 1)
            dve.wait_ge(norm_ok, TILES)
            G = TILES // 4
            for g in range(4):
                h = xs[:, G * g:G * (g + 1), :]
                nc.vector.tensor_scalar(h, h, 0.0, None, ALU.max).then_inc(h_ok, 1)
            for g in range(4):
                dve.wait_ge(stat_done, g + 1)
                last = nc.vector.tensor_tensor(stat_lo[:, G * g:G * (g + 1), :], xs[:, G * g:G * (g + 1), :],
                                               stat_hi[:, G * g:G * (g + 1), :].bitcast(f32), ALU.subtract)
            link(last)

            dve.wait_ge(w_in, 16 * W_LOADS)
            link(nc.vector.tensor_tensor(fl[:, :, :], dl[:, :, :], fl[:, :, :], ALU.mult))
            link(nc.vector.tensor_tensor(fl[:, :, :], fl[:, :, :], dl[:, :, :], ALU.mult))
            link(nc.vector.tensor_tensor(srow, fl[:, 0, :], fl[:, 1, :], ALU.add))
            nc.vector.tensor_tensor(srow, srow, fl[:, 2, :], ALU.add).then_inc(srow_ok, 1)
            dve.wait_ge(pe_setup, 1)
            nc.vector.tensor_copy(wT[:, :, :], one[0][:, 0:3 * D].rearrange("p (a d) -> p a d", a=3))\
              .then_inc(products_ok, 1)
            dve.wait_ge(pe_setup, 2)
            link(nc.vector.tensor_copy(g_hi[:, :], one[1][:, 0:D]))
            link(nc.vector.tensor_tensor(g_lo[:, :], one[1][:, 0:D], g_hi[:, :].bitcast(f32), ALU.subtract))
            link(nc.vector.tensor_copy(whg[:, :], one[1][:, D:2 * D]))
            nc.vector.tensor_copy(scale[:, :], one[1][:, 2 * D:2 * D + TILES]).then_inc(products_ok, 1)

            for g in range(TILES // 4):
                dve.wait_ge(key_hi_ok, g + 1)
                hi = key_columns(keyT_hi, g)
                lo = key_columns(keyT_lo, g)
                ps = one[2 + g % 2].rearrange("p (b q s) -> p b q s", b=4, q=NQ)
                nc.vector.tensor_tensor(lo, ps, hi.bitcast(f32), ALU.subtract).then_inc(keyT_done, 1)

            dve.wait_ge(resid_in, 16)

            def q_part(c):
                wait(dve, qh_ok, c + 1)
                nc.vector.tensor_tensor(q_lo, q_ps, q_hi.bitcast(f32), ALU.subtract).then_inc(q_split, 1)

            def score_part(c, h):
                wait(dve, pT_raw, PUNITS * (c - 1))
                for u in range(SUNITS):
                    wait(dve, sco_raw, SUNITS * c + u + 1)
                    t, g = u // (N // SG), u % (N // SG)
                    nq = SG // SEG
                    dst = scores[:, h, t, HALF * (g // 2):HALF * (g // 2 + 1)]\
                        .rearrange("p (b q s) -> p q b s", q=NQ, s=SQ)[:, nq * (g % 2):nq * (g % 2 + 1)]
                    src = sco_ps[u % 2][:, :].rearrange("p (q b s) -> p q b s", q=nq, s=SQ)
                    nc.vector.tensor_scalar(dst, src, -1.0, None,
                                            ALU.mult, ALU.min, accum_out=pmin[:, h, u:u + 1]).then_inc(sco_out, 1)
                wait(dve, sco_out, SUNITS * (c + 1))
                nc.vector.tensor_reduce(nmax[:, h, :], pmin[:, h, :].rearrange("p (t g) -> p t g", t=QT),
                                        AX.X, ALU.min).then_inc(max_ok, 1)

            def prob_part(c):
                for u in range(PUNITS):
                    n = PUNITS * c + u
                    wait(dve, pT_hi_ok, n + 1)
                    s = probT[:, u % NPT]
                    nc.vector.tensor_tensor(s[:, :, 1, :], pT_ps[u % 3].rearrange("p (k r) -> p k r", k=PK),
                                            s[:, :, 0, :].bitcast(f32), ALU.subtract).then_inc(pT_ok, 1)
                wait(dve, bt_half_ok, c + 1)
                nc.vector.tensor_tensor(btT, pv_ps[:, 0:QR], bt_half, ALU.add).then_inc(bt_ok, 1)

            def att_part(c, h, base):
                wait(dve, exp_ok, c + 1)
                count[0] = base
                link(nc.vector.reciprocal(coef[:, h, :], rsum[:, h, :]))
                link(nc.vector.tensor_scalar(coef[:, h, :], coef[:, h, :], gamma_sb[:, 0:1], None, ALU.mult))
                wait(dve, att_raw, c + 1)
                for t in range(QT):
                    r = tile_of(resid, QT * c + t)
                    last = nc.vector.scalar_tensor_tensor(r, pv_ps[:, D * t:D * (t + 1)], coef[:, h, t:t + 1], r,
                                                          ALU.mult, ALU.add)
                last.then_inc(att_ok, 1)

            base0 = count[0]
            q_part(0)
            score_part(0, 0)
            q_part(1)
            score_part(1, 1)
            q_part(2)
            prob_part(0)

            def step(c, h):
                score_part(c + 1, 1 - h)
                att_part(c - 1, 1 - h, base0 + 2 * (c - 1))
                q_part(c + 2)
                prob_part(c)
            with dve.Fori(1, QCH - 4, 2) as c:
                step(c, 1)
                step(c + 1, 0)
            c = QCH - 3
            step(c, 1)
            score_part(c + 2, 1)
            att_part(c, 1, base0 + 2 * c)
            prob_part(c + 1)
            att_part(c + 1, 0, base0 + 2 * (c + 1))
            prob_part(c + 2)
            att_part(c + 2, 1, base0 + 2 * (c + 2))
            dve.wait_ge(att_ok, QCH)

            def turn(v, u):
                n = UNITS * v + u
                l = u // LU
                if u % LU == 0:
                    wait(dve, adj_loaded[l], LOAD_INC * (v + 1))
                wait(dve, hi_ok, n - NT + 1)
                wait(dve, lo_pool, n - NT + 1)
                src = adj_in[l].rearrange("p (a b s) -> p b a s", a=BLOCKS, s=SQ)[:, UT * (u % LU):UT * (u % LU) + UT]
                dst = turned[u % NT].rearrange("p (b a s) -> p b a s", b=UT, s=SQ)
                nc.vector.transpose(dst, src).then_inc(adj_turned, 1)

            def low(v, u):
                n = UNITS * v + u
                wait(dve, hi_ok, n + 1)
                wait(dve, unit_done, n - NL + 1)
                nc.vector.tensor_tensor(adj_lo[u % NL][:, POOL_E:], turned[u % NT][:, POOL_E:],
                                        adj_hi[u % NH][:, POOL_E:].bitcast(f32), ALU.subtract).then_inc(lo_dve, 1)

            LN_LINKS = 1 + 5 + 1

            base_rows = count[0]

            def rows_first(c):
                count[0] = base_rows + LN_LINKS * c
                wait(dve, rows_raw, c + 1)
                r = resid[:, at(CT * c, CT), :]
                wait(dve, h2_raw, c)
                nc.vector.tensor_tensor(hn[:, :, :], row_ps.rearrange("p (t d) -> p t d", t=CT), r, ALU.add)\
                  .then_inc(rows_ok, 1)
                wait(dve, rows_ok, c + 1)
                for t in range(CT):
                    nc.vector.bn_stats(stats[:, t, :], hn[:, t, :])
                link(nc.vector.tensor_tensor(r, hn[:, :, :], bias_sb[:, :, :], ALU.add))
                mean_and_var(0, CT).then_inc(var2_ok, 1)

            def rows_second(c):
                count[0] = base_rows + LN_LINKS * c + 6
                wait(dve, std2_ok, c + 1)
                link(nc.vector.reciprocal(mom[:, 1, 0:CT], mom[:, 0, 0:CT]))
                for t in range(CT):
                    last = nc.vector.tensor_scalar(hn[:, t, :], hn[:, t, :], mom[:, 2, t:t + 1], mom[:, 1, t:t + 1],
                                                   ALU.subtract, ALU.mult)
                last.then_inc(hn_ok, 1)

            def add_y(k):
                wait(dve, acc_out, 2 * GC + k + 1)
                y = stacked_rows(yT, k)
                nc.vector.tensor_tensor(y, uT[:, :].rearrange("p (b s) -> p b s", s=SQ), y, ALU.add).then_inc(y_ok, 1)

            def add_part(k):
                wait(dve, part_raw, k + 1)
                r = resid[:, at(CT * k, CT), :]
                nc.vector.tensor_tensor(r, h2_ps.rearrange("p (t d) -> p t d", t=CT), r, ALU.add).then_inc(part_ok, 1)

            def rows_out(g, k):
                n = GC * (g - 4) + k
                wait(dve, rows_raw, 2 * GC + n + 1)
                wait(dve, stored, 16 * n)
                nc.vector.tensor_tensor(outb[:, :, :], row_ps.rearrange("p (t d) -> p t d", t=CT),
                                        resid[:, at(CT * (GC * GROUPS[g][0] + k), CT), :], ALU.add).then_inc(out_ready, 1)

            def restack(g, i):
                m = RG * g + i
                ps = st_ps[i % 2].rearrange("p (t d) -> p t d", t=RT)
                t0 = HT * GROUPS[g][0] + RT * i
                if g < 2:
                    dve.wait_ge(st_hi, m + 1)
                    nc.vector.tensor_tensor(xw_lo[:, t0:t0 + RT, :], ps, xw_hi[:, t0:t0 + RT, :].bitcast(f32),
                                            ALU.subtract).then_inc(st_lo, 1)
                else:
                    dve.wait_ge(st_raw, m + 1)
                    dve.wait_ge(st_lo, m)
                    for t in range(RT):
                        last = nc.vector.tensor_scalar(zrow[:, t, :], ps[:, t, :], scale[:, t0 + t:t0 + t + 1], None,
                                                       ALU.mult)
                    last.then_inc(z_ok, 1)
                    dve.wait_ge(st_hi, m + 1)
                    nc.vector.tensor_tensor(stat_lo[:, t0:t0 + RT, :], zrow[:, :, :],
                                            stat_hi[:, t0:t0 + RT, :].bitcast(f32), ALU.subtract).then_inc(st_lo, 1)

            def plan_of(after, g):
                if not after:
                    return []
                a, k = after
                first, second = {1: (4, 5), 2: (3, 3)}.get(g, (6, 8)) if a < g else (6, 8)
                plan = []
                if a < 2:
                    c = GC * a + k
                    plan = [(first, lambda: rows_first(c)), (second, lambda: rows_second(c))]
                elif a == 2:
                    plan = [(4, lambda: add_y(k))]
                elif a == 3:
                    plan = [(7, lambda: add_part(k))]
                else:
                    plan = [(6, lambda: rows_out(a, k))]
                if a < g and a < 4:
                    start, by = {0: (8, 1), 1: (3, 0), 2: (5, 1), 3: (6, 1)}[a]
                    plan += [(start + by * i, lambda i=i: restack(a, i)) for i in range(RG)]
                return plan

            turn(0, 0)

            def chunk(g, k, after):
                plan = plan_of(after, g)
                for j in range(len(GROUPS[g][1])):
                    v = visit_number(g, k, j)
                    for u in range(UNITS):
                        ahead(after, plan, UNITS * j + u)
                        if u < UNITS - 1:
                            turn(v, u + 1)
                        elif not (g == len(GROUPS) - 1 and isinstance(k, int) and k == GC - 1):
                            turn(v + 1, 0)
                        low(v, u)

            def flush(after):
                rows_out(*after)
            last = None
            for g in range(len(GROUPS)):
                chunk(g, 0, last)
                end = GC if g < len(GROUPS) - 1 else GC - 1
                with dve.Fori(1, end) as k:
                    chunk(g, k, (g, k - 1))
                if end < GC:
                    chunk(g, GC - 1, (g, GC - 2))
                last = (g, GC - 1)
            flush(last)

        @block.scalar
        def _(act):
            start_counts(act, "scalar")
            act.wait_ge(ident_ok, 2)
            act.wait_ge(var_ok, 1)
            nc.scalar.activation(mom[:, 0, :], mom[:, 5, :], ACT.Sqrt, bias=eps_sb[:, 0:1]).then_inc(std_ok, 1)
            G = TILES // 4
            for g in range(4):
                act.wait_ge(h_ok, g + 1)
                nc.scalar.activation(stat_hi[:, G * g:G * (g + 1), :], xs[:, G * g:G * (g + 1), :],
                                     ACT.Copy).then_inc(stat_done, 1)
            for g in range(TILES // 4):
                act.wait_ge(hT_ps, g + 1)
                hi = key_columns(keyT_hi, g)
                ps = one[2 + g % 2].rearrange("p (b q s) -> p b q s", b=4, q=NQ)
                nc.scalar.activation(hi, ps, ACT.Copy).then_inc(key_hi_ok, 1)

            def q_part(c):
                wait(act, q_raw, c + 1)
                wait(act, sco_raw, SUNITS * c)
                nc.scalar.activation(q_hi, q_ps, ACT.Copy).then_inc(qh_ok, 1)

            def exp_part(c, h):
                wait(act, max_ok, c + 1)
                for t in range(QT):
                    last = nc.scalar.activation(scores[:, h, t, :], scores[:, h, t, :], ACT.Exp,
                                                bias=nmax[:, h, t:t + 1], scale=-1.0, accum_out=rsum[:, h, t:t + 1])
                last.then_inc(exp_ok, 1)

            def prob_part(c):
                for u in range(PUNITS):
                    n = PUNITS * c + u
                    wait(act, pT_raw, n + 1)
                    wait(act, pv_unit, n - NPT + 1)
                    nc.scalar.activation(probT[:, u % NPT][:, :, 0, :],
                                         pT_ps[u % 3].rearrange("p (k r) -> p k r", k=PK), ACT.Copy)\
                      .then_inc(pT_hi_ok, 1)
                wait(act, pv_unit, PUNITS * (c + 1))
                nc.scalar.activation(bt_half, pv_ps[:, QR:2 * QR], ACT.Copy).then_inc(bt_half_ok, 1)

            q_part(0)
            q_part(1)
            exp_part(0, 0)

            def step(c, h):
                q_part(c + 2)
                prob_part(c)
                exp_part(c + 1, 1 - h)
            step(0, 0)
            with act.Fori(1, QCH - 4, 2) as c:
                step(c, 1)
                step(c + 1, 0)
            step(QCH - 3, 1)
            prob_part(QCH - 2)
            exp_part(QCH - 1, 1)
            prob_part(QCH - 1)

            def take(g, k):
                o = GC * g + k
                wait(act, unit_done, UNITS * (visit_number(g, k, len(GROUPS[g][1]) - 1) + 1))
                src = acc_ps[:, at(512 * (k % 2), 512)]
                if g == 3:
                    wait(act, st_raw, RG * 3)
                    nc.scalar.activation(stacked_rows(yT, k), src.rearrange("p (b s) -> p b s", s=SQ), ACT.Copy)\
                      .then_inc(acc_out, 1)
                    return
                if g < 2:
                    wait(act, rows_raw, o)
                elif g == 2:
                    wait(act, rows_raw, 2 * GC)
                    wait(act, y_ok, k)
                else:
                    wait(act, y_ok, GC)
                    wait(act, rows_raw, 2 * GC + GC * (g - 4) + k)
                nc.scalar.activation(uT[:, :], src, ACT.Copy).then_inc(acc_out, 1)

            def take_dual(g, k):
                src = dual_ps[:, at(512 * (k % 2), 512)]
                if g == 1:
                    dst, src = stacked_rows(yT, k), src.rearrange("p (b s) -> p b s", s=SQ)
                else:
                    dst = h2T[:, :]
                    wait(act, xw_raw, 2 * GC)
                    wait(act, part_raw, k)
                wait(act, unit_done, UNITS * (visit_number(g, k, len(GROUPS[g][1]) - 1) + 1))
                nc.scalar.activation(dst, src, ACT.Copy).then_inc(dual_out, 1)

            def std2(c):
                wait(act, var2_ok, c + 1)
                nc.scalar.activation(mom[:, 0, 0:CT], mom[:, 5, 0:CT], ACT.Sqrt, bias=eps_sb[:, 0:1]).then_inc(std2_ok, 1)

            def relu_out(c):
                wait(act, h2_raw, c + 1)
                wait(act, xw_raw, c)
                nc.scalar.activation(h2T[:, :], h2_ps, ACT.Relu).then_inc(h2T_ok, 1)

            def take_xw(g, k):
                wait(act, xw_raw, GC * g + k + 1)
                if g == 1:
                    wait(act, st_raw, RG)
                nc.scalar.activation(stacked_rows(xwT, k), xw_ps.rearrange("p (b s) -> p b s", s=SQ), ACT.Copy)\
                  .then_inc(xw_out, 1)

            def restack(g, i):
                m = RG * g + i
                t0 = HT * GROUPS[g][0] + RT * i
                if g < 2:
                    act.wait_ge(st_raw, m + 1)
                    nc.scalar.activation(xw_hi[:, t0:t0 + RT, :], st_ps[i % 2].rearrange("p (t d) -> p t d", t=RT),
                                         ACT.Copy).then_inc(st_hi, 1)
                else:
                    act.wait_ge(z_ok, m - 2 * RG + 1)
                    nc.scalar.activation(stat_hi[:, t0:t0 + RT, :], zrow[:, :, :], ACT.Copy).then_inc(st_hi, 1)

            def plan_of(after, g):
                if not after:
                    return []
                a, k = after
                c = GC * a + k
                if a < 2:
                    at_take, at_std, at_relu, at_xw = ({1: (2, 4, 6, 7), 2: (3, 3, 3, 3)}.get(g) if a < g
                                                       else (3, 7, 11, 13))
                    plan = [(at_take, lambda: take(a, k))]
                    if a == 1:
                        plan += [(at_take, lambda: take_dual(a, k))]
                    plan += [(at_std, lambda: std2(c)), (at_relu, lambda: relu_out(c)), (at_xw, lambda: take_xw(a, k))]
                elif a == 2:
                    plan = [(3, lambda: take(a, k))]
                elif a == 3:
                    plan = [(3, lambda: take(a, k)), (3, lambda: take_dual(a, k))]
                else:
                    plan = [(3, lambda: take(a, k))]
                if a < g and a < 4:
                    start, by = {0: (8, 1), 1: (3, 0), 2: (6, 1), 3: (7, 1)}[a]
                    plan += [(start + by * i, lambda i=i: restack(a, i)) for i in range(RG)]
                return plan

            def chunk(g, k, after):
                plan = plan_of(after, g)
                for j in range(len(GROUPS[g][1])):
                    for u in range(UNITS):
                        ahead(after, plan, UNITS * j + u)
                        n = UNITS * visit_number(g, k, j) + u
                        wait(act, adj_turned, n + 1)
                        wait(act, unit_done, n - NH + 1)
                        nc.scalar.activation(adj_hi[u % NH], turned[u % NT], ACT.Copy).then_inc(hi_ok, 1)
            passes(act, chunk, lambda after: take(*after))

        @block.tensor
        def _(pe):
            start_counts(pe, "tensor")
            mm, tr = nc.tensor.matmul, nc.tensor.transpose
            pe.wait_ge(ident_ok, 2)
            pe.wait_ge(w_in, 16 * W_LOADS)
            for i, w in enumerate((wl_sb, wr_sb, wh_sb)):
                last = tr(one[0][:, D * i:D * (i + 1)], w, ident[:, :])
            last.then_inc(pe_setup, 1)
            for g in range(TILES // 4):
                pe.wait_ge(h_ok, g // 2 + 1)
                wait(pe, keyT_done, g - 1)
                for b in range(4):
                    last = tr(one[2 + g % 2][:, P * b:P * (b + 1)], xs[:, 4 * g + b, :], ident[:, :])
                last.then_inc(hT_ps, 1)
                if g == 1:
                    pe.wait_ge(products_ok, 1)
                    pe.wait_ge(srow_ok, 1)
                    mm(one[1][:, 0:D], wT[:, 0, :], wT[:, 1, :], start=True, stop=True)
                    mm(one[1][:, D:2 * D], wT[:, 2, :], wg_sb, start=True, stop=True)
                    tr(one[1][:, 2 * D:2 * D + TILES], srow, ident[0:TILES, 0:TILES]).then_inc(pe_setup, 1)

            def queries(c):
                wait(pe, q_split, c)
                wait(pe, pT_ok, PUNITS * (c - 2))
                k_hi, k_lo = keyT_hi[:, at(QR * c, QR)], keyT_lo[:, at(QR * c, QR)]
                mm(q_ps, g_hi[:, :], k_hi, start=True, stop=False)
                mm(q_ps, g_hi[:, :], k_lo, start=False, stop=False)
                mm(q_ps, g_lo[:, :], k_hi, start=False, stop=True).then_inc(q_raw, 1)

            def score_part(c):
                wait(pe, q_split, c + 1)
                for u in range(SUNITS):
                    wait(pe, sco_out, SUNITS * c + u - 1)
                    t, g = u // (N // SG), u % (N // SG)
                    for a, k, s, e in ((q_hi, keyT_hi, True, False), (q_hi, keyT_lo, False, False),
                                       (q_lo, keyT_hi, False, True)):
                        for j in range(2):
                            col = SG * g + 512 * j
                            last = mm(sco_ps[u % 2][:, 512 * j:512 * (j + 1)], a[:, P * t:P * (t + 1)],
                                      k[:, col:col + 512], start=s, stop=e)
                    last.then_inc(sco_raw, 1)

            def prob_turn(c, h, u):
                n = PUNITS * c + u
                wait(pe, pT_ok, n - 2 if u >= 3 else PUNITS * c)
                if u == 2:
                    wait(pe, q_split, c + 3 if not isinstance(c, int) or c + 3 <= QCH else QCH)
                for k in range(PK):
                    for t in range(QT):
                        last = tr(pT_ps[u % 3][:, QR * k + P * t:QR * k + P * (t + 1)],
                                  stacked(scores[:, h, t, :], PK * u + k), ident[:, :])
                last.then_inc(pT_raw, 1)

            def prob_use(c, u):
                wait(pe, pT_ok, PUNITS * c + u + 1)
                for k in range(PK):
                    b = PK * u + k
                    s = probT[:, u % NPT, k]
                    both = s.rearrange("p h r -> p (h r)")
                    if b == 0:
                        mm(pv_ps, stat_hi[:, b, :], both, start=True, stop=False)
                        last = mm(pv_ps[:, 0:QR], stat_lo[:, b, :], s[:, 0, :], start=False, stop=False)
                    else:
                        mm(pv_ps[:, 0:QR], stat_lo[:, b, :], s[:, 0, :], start=False, stop=False)
                        last = mm(pv_ps, stat_hi[:, b, :], both, start=False, stop=b == TILES - 1)
                last.then_inc(pv_unit, 1)

            def prob_part(c, h):
                wait(pe, exp_ok, c + 1)
                prob_turn(c, h, 0)
                prob_turn(c, h, 1)
                prob_turn(c, h, 2)
                wait(pe, att_ok, c)
                for u in range(PUNITS):
                    prob_use(c, u)
                    if u + 3 < PUNITS:
                        prob_turn(c, h, u + 3)

            def att_rows(c):
                wait(pe, bt_ok, c + 1)
                for t in range(QT):
                    last = mm(pv_ps[:, D * t:D * (t + 1)], btT[:, P * t:P * (t + 1)], whg[:, :], start=True, stop=True)
                last.then_inc(att_raw, 1)

            pe.wait_ge(products_ok, 2)
            pe.wait_ge(keyT_done, TILES // 4)
            queries(0)
            score_part(0)
            queries(1)
            score_part(1)
            queries(2)
            prob_part(0, 0)

            def step(c, h):
                score_part(c + 1)
                att_rows(c - 1)
                queries(c + 2)
                prob_part(c, h)
            with pe.Fori(1, QCH - 4, 2) as c:
                step(c, 1)
                step(c + 1, 0)
            c = QCH - 3
            step(c, 1)
            score_part(c + 2)
            att_rows(c)
            prob_part(c + 1, 0)
            att_rows(c + 1)
            prob_part(c + 2, 1)
            att_rows(c + 2)

            stats_of = ((stat_hi, stat_lo), (stat_hi, stat_lo), (xw_hi, xw_lo), (xw_hi, xw_lo),
                        (stat_hi, stat_lo), (stat_hi, stat_lo))
            dual_stats_of = {1: (xw_hi, xw_lo), 3: (stat_hi, stat_lo)}

            def unit(g, k, j, u, acc, dual):
                n = UNITS * visit_number(g, k, j) + u
                cols = GROUPS[g][1]
                wait(pe, lo_pool, n + 1)
                wait(pe, lo_dve, n + 1)
                if isinstance(k, int) and k == 0 and g in (1, 3, 4) and j == 1:
                    wait(pe, st_lo, RG * {1: 0, 3: 2, 4: 3}[g] + UT * u // RT + 1)
                for b in range(UT):
                    t = HT * cols[j] + UT * u + b
                    hi, lo = adj_hi[u % NH][:, ROWS * b:ROWS * (b + 1)], adj_lo[u % NL][:, ROWS * b:ROWS * (b + 1)]
                    begin, end = u == 0 and b == 0, u == UNITS - 1 and b == UT - 1
                    if dual is not None:
                        s_hi, s_lo = dual_stats_of[g]
                        mm(dual, s_hi[:, t, :], hi, start=begin, stop=False)
                        mm(dual, s_hi[:, t, :], lo, start=False, stop=False)
                        mm(dual, s_lo[:, t, :], hi, start=False, stop=end)
                    s_hi, s_lo = stats_of[g]
                    mm(acc, s_hi[:, t, :], hi, start=begin and j == 0, stop=False)
                    mm(acc, s_hi[:, t, :], lo, start=False, stop=False)
                    last = mm(acc, s_lo[:, t, :], hi, start=False, stop=end and j == len(cols) - 1)
                last.then_inc(unit_done, 1)

            def sum_rows(g, k):
                wait(pe, acc_out, GC * g + k + 1)
                if g < 2:
                    wait(pe, rows_ok, GC * g + k)
                else:
                    wait(pe, out_ready, GC * (g - 4) + k)
                for t in range(CT):
                    last = tr(row_ps[:, P * t:P * (t + 1)], uT[:, P * t:P * (t + 1)], ident[:, :])
                last.then_inc(rows_raw, 1)

            def part_rows(k):
                wait(pe, dual_out, GC + k + 1)
                wait(pe, part_ok, k)
                for t in range(CT):
                    last = tr(h2_ps[:, P * t:P * (t + 1)], h2T[:, P * t:P * (t + 1)], ident[:, :])
                last.then_inc(part_raw, 1)

            def norm_cols(c):
                wait(pe, hn_ok, c + 1)
                wait(pe, h2T_ok, c)
                for t in range(CT):
                    last = tr(h2_ps[:, P * t:P * (t + 1)], hn[:, t, :], ident[:, :])
                last.then_inc(h2_raw, 1)

            def times_weight(c):
                wait(pe, h2T_ok, c + 1)
                wait(pe, xw_out, c)
                mm(xw_ps, w1_sb[:, :], h2T[:, :], start=True, stop=True).then_inc(xw_raw, 1)

            def restack(g, i):
                m = RG * g + i
                if i == 0:
                    if g < 2:
                        wait(pe, xw_out, GC * (g + 1))
                    elif g == 2:
                        wait(pe, y_ok, GC)
                    else:
                        wait(pe, acc_out, 4 * GC)
                wait(pe, st_lo, m - 1)
                for t in range(RT):
                    last = tr(st_ps[i % 2][:, P * t:P * (t + 1)], stacked(xwT if g < 2 else yT, RT * i + t), ident[:, :])
                last.then_inc(st_raw, 1)

            def plan_of(after, g):
                if not after:
                    return []
                a, k = after
                c = GC * a + k
                plan = []
                if a < 2:
                    at_rows, at_norm, at_weight = {1: (2, 5, 6), 2: (0, 0, 0)}.get(g) if a < g else (3, 8, 11)
                    plan = [(at_rows, lambda: sum_rows(a, k)), (at_norm, lambda: norm_cols(c)),
                            (at_weight, lambda: times_weight(c))]
                elif a == 3:
                    plan = [(5, lambda: part_rows(k))]
                elif a > 3:
                    plan = [(4, lambda: sum_rows(a, k))]
                if a < g and a < 4:
                    start, by = {0: (7, 1), 1: (0, 0), 2: (4, 1), 3: (5, 1)}[a]
                    plan += [(start + by * i, lambda i=i: restack(a, i)) for i in range(RG)]
                    if a == 1:
                        plan += [(0, lambda: pe.wait_ge(st_lo, 2 * RG))]
                return plan

            def chunk(g, k, after):
                plan = plan_of(after, g)
                acc = acc_ps[:, at(512 * (k % 2), 512)]
                wait(pe, acc_out, GC * g + k - 1)
                for j in range(len(GROUPS[g][1])):
                    dual = None
                    if GROUPS[g][2] and j == 1:
                        dual = dual_ps[:, at(512 * (k % 2), 512)]
                        wait(pe, dual_out, GC * (g // 2) + k - 1)
                    for u in range(UNITS):
                        ahead(after, plan, UNITS * j + u)
                        unit(g, k, j, u, acc, dual)
            passes(pe, chunk, lambda after: sum_rows(*after))


_INS = ['x', 'adj', 'L0_gnn_W_l', 'L0_gnn_W_r', 'L0_gnn_W_h', 'L0_gnn_W_g', 'L0_gnn_gamma', 'L1_gnn_d_list',
        'L1_gnn_weight', 'L1_gnn_filt', 'L1_gnn_bias']
_OUTS = [((4096, 128), 'float32')]


def kernel(**inputs):
    import numpy as _np
    import concourse.bacc as _bacc
    from concourse import mybir as _mybir
    from concourse.bass_utils import run_bass_kernel_spmd as _run

    nc = _bacc.Bacc("TRN2", target_bir_lowering=False, num_devices=1)
    arrays, args = {}, []
    for name in _INS:
        a = _np.ascontiguousarray(inputs[name])
        arrays[f"in_{name}_dram"] = a
        args.append(nc.dram_tensor(f"in_{name}_dram", a.shape, _mybir.dt.from_np(a.dtype), kind="ExternalInput").ap())
    for i, (shape, dtype) in enumerate(_OUTS):
        dt = _mybir.dt.from_np(_np.dtype(dtype))
        args.append(nc.dram_tensor(f"out_{i}_dram", shape, dt, kind="ExternalOutput").ap())
    preln_attention_graph_kernel(nc, *args)
    r = _run(nc, [arrays], core_ids=[0])
    return r.results[0]["out_0_dram"]
```

```python
import concourse.bass as bass
from concourse import mybir
from contextlib import ExitStack


def preln_attention_graph_kernel(nc, x, adj, w_l, w_r, w_h, w_g, gamma, d_list, weight, filt, bias, out):
    f32, f32r = mybir.dt.float32, mybir.dt.float32r
    ALU, ACT, AX = mybir.AluOpType, mybir.ActivationFunctionType, mybir.AxisListType

    N, D = x.shape
    P = 128
    SQ = 32
    NQ = P // SQ
    TILES = N // P
    HALF = N // 2
    SEG = HALF // NQ
    HT = TILES // 2
    EPS = 1e-5

    ROWS = 512
    BLOCKS = ROWS // SQ
    CT = ROWS // P
    GC = HALF // ROWS
    UT = 2
    UNITS = HT // UT
    UE = UT * ROWS
    LU = 4
    LOADS = UNITS // LU
    NT, NH, NL = 4, 8, 4
    LOAD_INC = 16 * NQ
    POOL_E = 640
    POOL_E_SINGLE = 768
    WHOLE = (1, 5)
    RT = 4
    RG = HT // RT
    GROUPS = ((0, (0, 1), False),
              (1, (1, 0), True),
              (1, (1,), False),
              (0, (0, 1), True),
              (1, (1, 0), False),
              (0, (0,), False))
    DUAL = [[x[2] and j == len(x[1]) - 1 for j in range(len(x[1]))] for x in GROUPS]
    FIRST_VISIT = [GC * sum(len(x[1]) for x in GROUPS[:g]) for g in range(len(GROUPS))]

    QR = 256
    QCH = N // QR
    QT = QR // P
    SG = 1024
    SUNITS = QT * (N // SG)
    PK = 2
    PUNITS = TILES // PK
    NPT = 4
    HU = PUNITS // 2
    TURN_AHEAD, HI_AHEAD = 4, 2
    EXP_AT = (1, 2, 3, 4, 6, 7, 8, 9)
    SCORE_AT = (3, 5, 6, 8, 9, 11, 12, 14)
    EXPS = len(EXP_AT)

    ctx = ExitStack()
    with ctx:
        def sb(name, shape, dt=f32):
            return ctx.enter_context(nc.sbuf_tensor(name, shape, dt))

        def sem(name):
            return ctx.enter_context(nc.semaphore(name))

        stat_hi = sb("stat_hi", [P, TILES, D], f32r)
        stat_lo = sb("stat_lo", [P, TILES, D], f32r)
        keys = sb("keys", [P, 2 * N], f32r)
        resid = sb("resid", [P, TILES, D])
        split = sb("split", [P, 2 * QT * HALF + NPT * PK * 2 * QR + 2 * QR], f32r)
        raw = sb("raw", [P, 2 * QT * N])
        keyT_hi, keyT_lo = keys[:, 0:N], keys[:, N:2 * N]
        moved = split[:, 0:2 * QT * HALF].rearrange("p (h x) -> p h x", h=2)
        p0 = 2 * QT * HALF
        probT = split[:, p0:p0 + NPT * PK * 2 * QR].rearrange("p (n k h r) -> p n k h r", n=NPT, k=PK, h=2)
        q0 = p0 + NPT * PK * 2 * QR
        q_hi = split[:, q0:q0 + QR]
        q_lo = split[:, q0 + QR:q0 + 2 * QR]
        scores = raw[:, :].rearrange("p (n t k) -> p n t k", n=2, t=QT)
        xw_hi = keyT_hi.rearrange("p (t d) -> p t d", d=D)
        xw_lo = keyT_lo.rearrange("p (t d) -> p t d", d=D)
        adj_hi = [split[:, i * UE:(i + 1) * UE] for i in range(NH)]
        adj_lo = [split[:, (NH + i) * UE:(NH + i + 1) * UE] for i in range(NL)]
        LE = LU * UE
        adj_in = [raw[:, 0:LE], raw[:, 2 * LE:3 * LE]]
        turned = [raw[:, LE + i * UE:LE + (i + 1) * UE] for i in range(NT)]
        xwT = raw[:, 3 * LE:3 * LE + HALF]
        yT = raw[:, 3 * LE + HALF:3 * LE + 2 * HALF]
        xs = raw[:, 0:TILES * D].rearrange("p (t d) -> p t d", d=D)
        w0 = TILES * D
        wl_sb, wr_sb, wh_sb, wg_sb = (raw[:, w0 + i * D:w0 + (i + 1) * D] for i in range(4))
        wT = raw[:, w0 + 4 * D:w0 + 7 * D].rearrange("p (a d) -> p a d", a=3)
        dl = raw[0:TILES, w0 + 7 * D:w0 + 10 * D].rearrange("p (a d) -> p a d", a=3)
        fl = raw[0:TILES, w0 + 10 * D:w0 + 13 * D].rearrange("p (a d) -> p a d", a=3)
        srow = raw[0:TILES, w0 + 13 * D:w0 + 14 * D]

        ident = sb("ident", [P, P])
        whg = sb("whg", [P, D])
        w1_sb = whg
        g_hi = sb("g_hi", [P, D], f32r)
        g_lo = sb("g_lo", [P, D], f32r)
        bias_sb = sb("bias_sb", [P, CT, D])
        scale = sb("scale", [P, TILES])
        stats = sb("stats", [P, TILES, 6])
        mom = sb("mom", [P, 6, TILES])
        small = sb("small", [P, 2 * (SUNITS + EXPS + 3 * QT) + 2])
        pmin, rpart = (small[:, 2 * SUNITS * i:2 * SUNITS * (i + 1)].rearrange("p (h e) -> p h e", h=2) for i in range(2))
        s0 = 2 * (SUNITS + EXPS)
        nmax, rsum, coef = (small[:, s0 + 2 * QT * i:s0 + 2 * QT * (i + 1)].rearrange("p (h t) -> p h t", h=2)
                            for i in range(3))
        gamma_sb, eps_sb = small[:, s0 + 6 * QT:s0 + 6 * QT + 1], small[:, s0 + 6 * QT + 1:s0 + 6 * QT + 2]
        uT = sb("uT", [P, ROWS])
        bt_half, btT = uT[:, 0:QR], uT[:, QR:2 * QR]
        hn = sb("hn", [P, CT, D])
        zrow = hn
        h2T = sb("h2T", [P, ROWS])
        outb = sb("outb", [P, CT, D])
        turned_p = [t[:, :, :].rearrange("p t d -> p (t d)") for t in (hn, outb, bias_sb)] + [h2T[:, :]]
        WT = UT * len(WHOLE)
        xwT_tiles, yT_tiles = (t[:, 0:WT * D].rearrange("p (t d) -> p t d", d=D) for t in (xwT, yT))
        h_whole = [yT_tiles, outb]
        xw_whole = [xwT_tiles, outb]
        z_whole = [xwT_tiles, bias_sb]

        bank = [ctx.enter_context(nc.psum_tensor(f"bank{i}", [P, 2 * 512], f32)) for i in range(4)]
        sco_ps = [bank[0], bank[1]]
        pv_ps = [bank[2][:, 0:512], bank[2][:, 512:1024]]
        q_ps = bank[3][:, 0:QR]
        att_ps = bank[3][:, 512:512 + QT * D]
        one = [bank[i // 2][:, 512 * (i % 2):512 * (i % 2) + 512] for i in range(8)]
        acc_ps, dual_ps = bank[0], bank[1]
        row_ps, h2_ps, xw_ps = one[4], one[5], one[6]
        st_ps = [one[7], one[6]]

        x_in = [sem(f"x_in{i}") for i in range(2)]; resid_in = sem("resid_in"); w_in = sem("w_in")
        ident_set = sem("ident_set"); ident_ok = sem("ident_ok")
        dve_step = sem("dve_step")
        stats_ok = sem("stats_ok"); norm_ok = sem("norm_ok"); rstd_ok = sem("rstd_ok"); h_low = sem("h_low")
        early_ok = sem("early_ok"); srow_ok = sem("srow_ok"); products_ok = sem("products_ok")
        key_hi_ok = sem("key_hi_ok")
        pe_setup = sem("pe_setup")
        var_ok = sem("var_ok"); std_ok = sem("std_ok")
        h_ok = sem("h_ok"); hT_ps = sem("hT_ps"); keyT_done = sem("keyT_done"); stat_done = sem("stat_done")
        q_raw = sem("q_raw"); q_split = sem("q_split"); qh_ok = sem("qh_ok")
        sco_raw = sem("sco_raw"); sco_out = sem("sco_out"); max_ok = sem("max_ok"); exp_ok = sem("exp_ok")
        p_moved = [sem(f"p_moved{i}") for i in range(2)]
        p_turned = sem("p_turned"); rsum_ok = sem("rsum_ok"); pT_dve = sem("pT_dve"); late_in = sem("late_in")
        pT_hi_ok = sem("pT_hi_ok"); pT_ok = sem("pT_ok"); pv_unit = sem("pv_unit")
        bt_half_ok = sem("bt_half_ok"); bt_ok = sem("bt_ok"); att_raw = sem("att_raw"); att_ok = sem("att_ok")
        adj_loaded = [sem(f"adj_loaded{i}") for i in range(LOADS)]
        adj_turned = sem("adj_turned"); hi_ok = sem("hi_ok"); lo_dve = sem("lo_dve"); lo_pool = sem("lo_pool")
        unit_done = sem("unit_done")
        acc_out = sem("acc_out"); dual_out = sem("dual_out"); rows_raw = sem("rows_raw"); rows_ok = sem("rows_ok")
        var2_ok = sem("var2_ok"); std2_ok = sem("std2_ok"); hn_ok = sem("hn_ok")
        h2_raw = sem("h2_raw"); h2T_ok = sem("h2T_ok"); xw_raw = sem("xw_raw"); xw_out = sem("xw_out")
        y_ok = sem("y_ok"); part_raw = sem("part_raw"); part_ok = sem("part_ok")
        whole_ok = sem("whole_ok")
        st_raw = sem("st_raw"); z_ok = sem("z_ok"); st_hi = sem("st_hi"); st_lo = sem("st_lo")
        out_ready = sem("out_ready"); stored = sem("stored")

        from_one = {"scalar": (acc_out, dual_out, h2T_ok, xw_out), "tensor": (rows_raw, h2_raw, part_raw, xw_raw),
                    "vector": (bt_ok, att_ok, rows_ok, y_ok, part_ok, out_ready), "sync": (stored,)}

        def start_counts(eng, name):
            for s in from_one[name]:
                eng.sem_inc(s, 1)
            if name == "vector":
                eng.sem_inc(p_turned, PUNITS)

        def wait(eng, s, value):
            if isinstance(value, int) and value <= 0:
                return
            eng.wait_ge(s, value + 1 if any(s is x for xs_ in from_one.values() for x in xs_) else value)

        def passes(eng, chunk, flush):
            last = None
            for g in range(len(GROUPS)):
                chunk(g, 0, last)
                with eng.Fori(1, GC) as k:
                    chunk(g, k, (g, k - 1))
                last = (g, GC - 1)
            flush(last)

        def is_early(g, k, j):
            return isinstance(k, int) and (g, k, j) == (3, 0, 0)

        def visits(g, k):
            mine = [(g, k, j) for j in range(len(GROUPS[g][1])) if not is_early(g, k, j)]
            return [(3, 0, 0)] + mine if isinstance(k, int) and (g, k) == (2, 0) else mine

        def visit_number(g, k, j):
            if is_early(g, k, j):
                return FIRST_VISIT[2]
            return FIRST_VISIT[g] + len(GROUPS[g][1]) * k + j + (1 if g == 2 else 0)

        def is_whole(g, k, j, u):
            return u in WHOLE and not DUAL[g][j] and not is_early(g, k, j)

        def split_count(g, k, j, u):
            return 2 if u and is_whole(g, k, j, u - 1) else 1

        def ahead(before, plan, u):
            for pos, step in plan:
                if pos == u:
                    step()

        def at(c, size):
            return slice(c, c + size) if isinstance(c, int) else bass.ds(c, size)

        def stacked(t2d, b):
            return t2d[:, P * b:P * (b + 1)]

        def key_columns(kT, g):
            v = kT.rearrange("p (h q b s) -> p h b q s", h=2, q=NQ, s=SQ)
            return v[:, g // (HT // 4), 4 * (g % (HT // 4)):4 * (g % (HT // 4)) + 4]

        def stacked_rows(yh, q):
            return yh.rearrange("p (b q s) -> p q b s", q=NQ, s=SQ)[:, at(q, 1)].rearrange("p q b s -> p (q b) s")

        def tile_of(t3d, t):
            return t3d[:, t, :] if isinstance(t, int) else t3d[:, bass.ds(t, 1), :].rearrange("p a d -> p (a d)")

        W_LOADS = 4 + 1 + 2 * 2 * NQ
        LATE_LOADS = CT + 1
        MOVE_INC = 16 * NQ * NQ

        block = ctx.enter_context(nc.Block())

        @block.sync
        def _(sp):
            start_counts(sp, "sync")
            xq = x.rearrange("(h q b s) d -> h q s b d", h=2, q=NQ, s=SQ)
            for h in range(2):
                for q in range(NQ):
                    sp.dma_start(xs[SQ * q:SQ * (q + 1), HT * h:HT * (h + 1), :], xq[h, q]).then_inc(x_in[h], 16)
            for t, w in ((wl_sb, w_l), (wr_sb, w_r), (wh_sb, w_h), (wg_sb, w_g)):
                sp.dma_start(t, w[:, :]).then_inc(w_in, 16)
            sp.dma_start(gamma_sb[:, :], gamma[None, :].to_broadcast([P, 1])).then_inc(w_in, 16)
            for t, w in ((dl, d_list), (fl, filt)):
                for h in range(2):
                    for q in range(NQ):
                        sp.dma_start(t[HT * h:HT * (h + 1), :, SQ * q:SQ * (q + 1)],
                                     w.rearrange("j (h q b s) -> h q b j s", h=2, q=NQ, s=SQ)[h, q]).then_inc(w_in, 16)
            sp.dma_start(resid[:, :, :], x.rearrange("(t p) d -> p t d", p=P)).then_inc(resid_in, 16)

            def move(c, h):
                for i in range(2):
                    wait(sp, exp_ok, PUNITS * c + HU * (i + 1))
                    wait(sp, p_turned, PUNITS * c + HU * (i + 1))
                    for a in range(NQ):
                        for q in range(NQ):
                            src = scores[SQ * a:SQ * (a + 1), h, :, HALF * i + SEG * q:HALF * i + SEG * (q + 1)]
                            dst = moved[SQ * q:SQ * (q + 1), i].rearrange("s (t a w) -> s t a w", t=QT, a=NQ)
                            sp.dma_start(dst[:, :, a].bitcast(f32), src).then_inc(p_moved[i], 16)

            def late_loads():
                wait(sp, att_raw, QCH)
                sp.dma_start(w1_sb[:, :], weight[:, :]).then_inc(late_in, 16)
                sp.wait_ge(pT_ok, PUNITS * QCH)
                sp.wait_ge(pT_dve, 2 * PUNITS)
                for t in range(CT):
                    sp.dma_start(bias_sb[:, t, :], bias[None, :].to_broadcast([P, D])).then_inc(late_in, 16)

            move(0, 0)
            move(1, 1)
            with sp.Fori(2, QCH - 1, 2) as c:
                move(c, 0)
                move(c + 1, 1)

            av = adj.rearrange("(c a r) (h q l w) -> q h c l r a w", a=BLOCKS, r=SQ, h=2, q=NQ, l=LOADS)
            def load(g, k, j, l, rows):
                cols = GROUPS[g][1]
                v = visit_number(g, k, j)
                if isinstance(v, int) and v == 0:
                    for i in range(2):
                        sp.wait_ge(p_moved[i], MOVE_INC * (QCH - 1 + l))
                else:
                    wait(sp, adj_turned, UNITS * v + LU * l - (LOADS - 1) * LU)
                dst = adj_in[l].rearrange("p (a w) -> p a w", a=BLOCKS)
                for q in reversed(range(NQ)):
                    src = av[q, cols[j], at(rows, 1), l]
                    sp.dma_start(dst[SQ * q:SQ * (q + 1)], src.rearrange("c r a w -> (c r) a w"))\
                      .then_inc(adj_loaded[l], 16)

            def chunk(g, k, after):
                for vg, vk, j in visits(g, k):
                    rows = GC * GROUPS[vg][0] + vk
                    for l in range(LOADS):
                        load(vg, vk, j, l, rows)
                    if not after and j == 0:
                        late_loads()
            passes(sp, chunk, lambda after: None)
            wait(sp, stored, 16 * 2 * GC)

        @block.gpsimd
        def _(pool):
            nc.gpsimd.memset(eps_sb[:, :], EPS).then_inc(ident_ok, 1)
            nc.gpsimd.memset(ident[:, :], 0.0).then_inc(ident_set, 1)
            pool.wait_ge(ident_set, 1)
            nc.gpsimd.affine_select(out=ident[:, :], in_=ident[:, :], compare_op=ALU.not_equal, fill=1.0,
                                    base=0, pattern=[[-1, P]], channel_multiplier=1).then_inc(ident_ok, 1)

            def add_whole(dst, hi, lo, half):
                for w, u in enumerate(WHOLE):
                    t = HT * half + UT * u
                    nc.gpsimd.tensor_tensor(dst[half][:, UT * w:UT * (w + 1), :], hi[:, t:t + UT, :].bitcast(f32),
                                            lo[:, t:t + UT, :].bitcast(f32), ALU.add).then_inc(whole_ok, 1)


            def prob_low(c, tiles):
                for u in range(PUNITS):
                    wait(pool, pT_hi_ok, PUNITS * c + u + 1)
                    s = probT[:, u % NPT, 0:tiles]
                    nc.gpsimd.tensor_tensor(s[:, :, 1, :],
                                            turned_p[u % NPT].rearrange("p (k r) -> p k r", k=PK)[:, 0:tiles],
                                            s[:, :, 0, :].bitcast(f32), ALU.subtract).then_inc(pT_ok, 1)
            prob_low(0, PK)
            with pool.Fori(1, QCH - 2) as c:
                prob_low(c, PK)
            prob_low(QCH - 2, 1)
            prob_low(QCH - 1, 1)
            for i in range(2):
                pool.wait_ge(p_moved[i], MOVE_INC * QCH)
            add_whole(h_whole, stat_hi, stat_lo, 0)
            pool.wait_ge(pT_ok, PUNITS * QCH)
            pool.wait_ge(pT_dve, 2 * PUNITS)
            add_whole(h_whole, stat_hi, stat_lo, 1)

            def chunk(g, k, after):
                for vg, vk, j in visits(g, k):
                    e = POOL_E if DUAL[vg][j] else POOL_E_SINGLE
                    for u in range(UNITS):
                        if vg == 2 and isinstance(k, int) and u == UNITS - 1:
                            pool.wait_ge(st_lo, 2 * RG)
                            add_whole(xw_whole, xw_hi, xw_lo, 0)
                        if is_whole(vg, vk, j, u):
                            continue
                        n = UNITS * visit_number(vg, vk, j) + u
                        wait(pool, hi_ok, n + 1)
                        wait(pool, unit_done, n - NL + 1)
                        nc.gpsimd.tensor_tensor(adj_lo[u % NL][:, 0:e], turned[u % NT][:, 0:e],
                                                adj_hi[u % NH][:, 0:e].bitcast(f32), ALU.subtract)\
                          .then_inc(lo_pool, split_count(vg, vk, j, u))
            passes(pool, chunk, lambda after: None)

        @block.vector
        def _(dve):
            start_counts(dve, "vector")
            count = [0]

            def link(ins):
                count[0] = count[0] + 1
                ins.then_inc(dve_step, 1)
                dve.wait_ge(dve_step, count[0])

            def mean_and_var(t0, t1):
                m = [mom[:, i, t0:t1] for i in range(6)]
                s = stats[:, t0:t1, :]
                link(nc.vector.tensor_tensor(m[0], s[:, :, 1], s[:, :, 4], ALU.add))
                link(nc.vector.tensor_tensor(m[1], s[:, :, 1], s[:, :, 4], ALU.subtract))
                link(nc.vector.tensor_tensor(m[3], s[:, :, 2], s[:, :, 5], ALU.add))
                link(nc.vector.tensor_scalar(m[2], m[0], 0.5, None, ALU.mult))
                link(nc.vector.scalar_tensor_tensor(m[4], m[1], 0.25, m[1], ALU.mult, ALU.mult))
                return nc.vector.scalar_tensor_tensor(m[5], m[3], 1.0 / D, m[4], ALU.mult, ALU.add)

            for h in range(2):
                dve.wait_ge(x_in[h], 16 * NQ)
                with dve.Fori(HT * h, HT * (h + 1) - 7, 8) as t0:
                    for t in range(8):
                        nc.vector.bn_stats(tile_of(stats, t0 + t), tile_of(xs, t0 + t)).then_inc(stats_ok, 1)
            dve.wait_ge(stats_ok, TILES)
            mean_and_var(0, TILES).then_inc(var_ok, 1)
            dve.wait_ge(w_in, 16 * W_LOADS)
            link(nc.vector.tensor_tensor(fl[:, :, :], dl[:, :, :], fl[:, :, :], ALU.mult))
            link(nc.vector.tensor_tensor(fl[:, :, :], fl[:, :, :], dl[:, :, :], ALU.mult))
            link(nc.vector.tensor_tensor(srow, fl[:, 0, :], fl[:, 1, :], ALU.add))
            nc.vector.tensor_tensor(srow, srow, fl[:, 2, :], ALU.add).then_inc(srow_ok, 1)
            dve.wait_ge(pe_setup, 1)
            nc.vector.tensor_copy(wT[:, :, :], one[0][:, 0:3 * D].rearrange("p (a d) -> p a d", a=3))\
              .then_inc(products_ok, 1)

            dve.wait_ge(std_ok, 1)
            link(nc.vector.reciprocal(mom[:, 1, :], mom[:, 0, :]))
            nc.vector.scalar_tensor_tensor(mom[:, 3, :], mom[:, 2, :], -1.0, mom[:, 1, :], ALU.mult, ALU.mult)\
              .then_inc(rstd_ok, 1)
            with dve.Fori(0, HT - 7, 8) as t0:
                for t in range(8):
                    nc.vector.tensor_scalar(tile_of(xs, t0 + t), tile_of(xs, t0 + t), mom[:, 2, at(t0 + t, 1)],
                                            mom[:, 1, at(t0 + t, 1)], ALU.subtract, ALU.mult).then_inc(norm_ok, 1)
            dve.wait_ge(norm_ok, HT)
            G = TILES // 4
            for g in range(2):
                h = xs[:, G * g:G * (g + 1), :]
                nc.vector.tensor_scalar(h, h, 0.0, None, ALU.max).then_inc(h_ok, 1)
            for g in range(4):
                dve.wait_ge(stat_done, g + 1)
                last = nc.vector.tensor_tensor(stat_lo[:, G * g:G * (g + 1), :], xs[:, G * g:G * (g + 1), :],
                                               stat_hi[:, G * g:G * (g + 1), :].bitcast(f32), ALU.subtract)
            link(last)

            dve.wait_ge(pe_setup, 2)
            link(nc.vector.tensor_copy(g_hi[:, :], one[1][:, 0:D]))
            link(nc.vector.tensor_tensor(g_lo[:, :], one[1][:, 0:D], g_hi[:, :].bitcast(f32), ALU.subtract))
            link(nc.vector.tensor_copy(whg[:, :], one[1][:, D:2 * D]))
            nc.vector.tensor_copy(scale[:, :], one[1][:, 2 * D:2 * D + TILES]).then_inc(products_ok, 1)

            for g in range(TILES // 4):
                dve.wait_ge(key_hi_ok, g + 1)
                hi = key_columns(keyT_hi, g)
                lo = key_columns(keyT_lo, g)
                ps = one[2 + g % 4].rearrange("p (b q s) -> p b q s", b=4, q=NQ)
                nc.vector.tensor_tensor(lo, ps, hi.bitcast(f32), ALU.subtract).then_inc(keyT_done, 1)

            dve.wait_ge(resid_in, 16)

            def q_part(c):
                wait(dve, qh_ok, c + 1)
                nc.vector.tensor_tensor(q_lo, q_ps, q_hi.bitcast(f32), ALU.subtract).then_inc(q_split, 1)

            def score_move(c, h, u):
                t, g = u // (N // SG), u % (N // SG)
                if u == 0:
                    for i in range(2):
                        wait(dve, p_moved[i], MOVE_INC * (c - 1))
                wait(dve, sco_raw, SUNITS * c + u + 1)
                nc.vector.tensor_scalar(scores[:, h, t, SG * g:SG * (g + 1)], sco_ps[u % 2][:, :], -1.0, None,
                                        ALU.mult, ALU.min, accum_out=pmin[:, h, u:u + 1]).then_inc(sco_out, 1)
                if u == SUNITS - 1:
                    wait(dve, sco_out, SUNITS * (c + 1))
                    wait(dve, exp_ok, PUNITS * (c - 1))
                    nc.vector.tensor_reduce(nmax[:, h, :], pmin[:, h, :].rearrange("p (t g) -> p t g", t=QT),
                                            AX.X, ALU.min).then_inc(max_ok, 1)

            def prob_turn(c, u):
                i = u // HU
                if u % HU == 0:
                    wait(dve, p_moved[i], MOVE_INC * (c + 1))
                wait(dve, pT_ok, PUNITS * c + u - NPT + 1)
                if isinstance(c, int) and c >= QCH - 2:
                    wait(dve, pT_dve, PUNITS * (c - (QCH - 2)) + u - NPT + 1)
                src = moved[:, i].bitcast(f32).rearrange("p (a b s) -> p b a s", a=QT * NQ, s=SQ)
                nc.vector.transpose(turned_p[u % NPT].rearrange("p (k a s) -> p k a s", k=PK, s=SQ),
                                    src[:, PK * (u % HU):PK * (u % HU) + PK]).then_inc(p_turned, 1)

            def prob_low(c, u):
                wait(dve, pT_hi_ok, PUNITS * c + u + 1)
                s = probT[:, u % NPT, 1]
                nc.vector.tensor_tensor(s[:, 1, :], turned_p[u % NPT][:, QR:2 * QR], s[:, 0, :].bitcast(f32),
                                        ALU.subtract).then_inc(pT_dve, 1)

            def bt_part(c, h):
                wait(dve, bt_half_ok, c + 1)
                nc.vector.tensor_tensor(btT, pv_ps[h][:, 0:QR], bt_half, ALU.add).then_inc(bt_ok, 1)

            def coef_part(c, h, base):
                wait(dve, exp_ok, PUNITS * (c + 1))
                nc.vector.tensor_reduce(rsum[:, h, :], rpart[:, h, :].rearrange("p (i t g) -> p t i g", i=2, t=QT),
                                        AX.XY, ALU.add).then_inc(rsum_ok, 1)
                wait(dve, rsum_ok, c + 1)
                count[0] = base
                link(nc.vector.reciprocal(coef[:, h, :], rsum[:, h, :]))
                link(nc.vector.tensor_scalar(coef[:, h, :], coef[:, h, :], gamma_sb[:, 0:1], None, ALU.mult))

            def att_part(c, h):
                wait(dve, att_raw, c + 1)
                for t in range(QT):
                    r = tile_of(resid, QT * c + t)
                    last = nc.vector.scalar_tensor_tensor(r, att_ps[:, D * t:D * (t + 1)], coef[:, h, t:t + 1], r,
                                                          ALU.mult, ALU.add)
                last.then_inc(att_ok, 1)

            base0 = count[0]
            LINKS = 2

            def scores_alone(c):
                q_part(c)
                for u in range(SUNITS):
                    score_move(c, c % 2, u)

            def step(c, h, more_scores=True, more_probs=True, before=True):
                for u in range(PUNITS):
                    if u == 0:
                        coef_part(c, h, base0 + LINKS * c)
                    if u == 1 and more_scores:
                        q_part(c + 2)
                    if u == 2 and before:
                        bt_part(c - 1, 1 - h)
                    if u == 8 and before:
                        att_part(c - 1, 1 - h)
                    if u == 0 and more_probs and not more_scores:
                        prob_low(c, 0)
                    if u + TURN_AHEAD < PUNITS:
                        prob_turn(c, u + TURN_AHEAD)
                    elif more_probs:
                        prob_turn(c + 1, u + TURN_AHEAD - PUNITS)
                    if not more_scores:
                        if u + 1 < PUNITS:
                            prob_low(c, u + 1)
                        elif more_probs:
                            prob_low(c + 1, 0)
                    if u in SCORE_AT and more_scores:
                        score_move(c + 2, h, SCORE_AT.index(u))

            scores_alone(0)
            scores_alone(1)
            for u in range(TURN_AHEAD):
                prob_turn(0, u)
            step(0, 0, before=False)
            with dve.Fori(1, QCH - 4, 2) as c:
                step(c, 1)
                step(c + 1, 0)
            step(QCH - 3, 1)
            step(QCH - 2, 0, more_scores=False)
            step(QCH - 1, 1, more_scores=False, more_probs=False)

            def end_of_attention():
                bt_part(QCH - 1, 1)
                att_part(QCH - 1, 1)
                wait(dve, att_ok, QCH)

            def turn(v, u):
                n = UNITS * v + u
                l = u // LU
                if u % LU == 0:
                    wait(dve, adj_loaded[l], LOAD_INC * (v + 1))
                if u in WHOLE:
                    wait(dve, unit_done, n - NT + 1)
                else:
                    wait(dve, hi_ok, n - NT + 1)
                    wait(dve, lo_pool, n - NT + 1)
                    wait(dve, lo_dve, n - NT + 1)
                src = adj_in[l].rearrange("p (a b s) -> p b a s", a=BLOCKS, s=SQ)[:, UT * (u % LU):UT * (u % LU) + UT]
                dst = turned[u % NT].rearrange("p (b a s) -> p b a s", b=UT, s=SQ)
                nc.vector.transpose(dst, src).then_inc(adj_turned, 1)

            def low(g, k, j, v, u):
                n = UNITS * v + u
                e = POOL_E if DUAL[g][j] else POOL_E_SINGLE
                wait(dve, hi_ok, n + 1)
                wait(dve, unit_done, n - NL + 1)
                nc.vector.tensor_tensor(adj_lo[u % NL][:, e:], turned[u % NT][:, e:],
                                        adj_hi[u % NH][:, e:].bitcast(f32), ALU.subtract)\
                  .then_inc(lo_dve, split_count(g, k, j, u))

            LN_LINKS = 1 + 5 + 1

            base_rows = count[0]

            def rows_first(c):
                count[0] = base_rows + LN_LINKS * c
                wait(dve, rows_raw, c + 1)
                r = resid[:, at(CT * c, CT), :]
                if isinstance(c, int) and c == 0:
                    dve.wait_ge(late_in, 16 * LATE_LOADS)
                wait(dve, h2_raw, c)
                nc.vector.tensor_tensor(hn[:, :, :], row_ps.rearrange("p (t d) -> p t d", t=CT), r, ALU.add)\
                  .then_inc(rows_ok, 1)
                wait(dve, rows_ok, c + 1)
                for t in range(CT):
                    nc.vector.bn_stats(stats[:, t, :], hn[:, t, :])
                link(nc.vector.tensor_tensor(r, hn[:, :, :], bias_sb[:, :, :], ALU.add))
                mean_and_var(0, CT).then_inc(var2_ok, 1)

            def rows_second(c):
                count[0] = base_rows + LN_LINKS * c + 6
                wait(dve, std2_ok, c + 1)
                link(nc.vector.reciprocal(mom[:, 1, 0:CT], mom[:, 0, 0:CT]))
                for t in range(CT):
                    last = nc.vector.tensor_scalar(hn[:, t, :], hn[:, t, :], mom[:, 2, t:t + 1], mom[:, 1, t:t + 1],
                                                   ALU.subtract, ALU.mult)
                last.then_inc(hn_ok, 1)

            def add_y(k):
                wait(dve, acc_out, 2 * GC + k + 1)
                y = stacked_rows(yT, k)
                nc.vector.tensor_tensor(y, uT[:, :].rearrange("p (b s) -> p b s", s=SQ), y, ALU.add).then_inc(y_ok, 1)

            def add_part(k):
                wait(dve, part_raw, k + 1)
                r = resid[:, at(CT * k, CT), :]
                nc.vector.tensor_tensor(r, h2_ps.rearrange("p (t d) -> p t d", t=CT), r, ALU.add).then_inc(part_ok, 1)

            def rows_out(g, k):
                n = GC * (g - 4) + k
                wait(dve, rows_raw, 2 * GC + n + 1)
                wait(dve, stored, 16 * n)
                nc.vector.tensor_tensor(outb[:, :, :], row_ps.rearrange("p (t d) -> p t d", t=CT),
                                        resid[:, at(CT * (GC * GROUPS[g][0] + k), CT), :], ALU.add).then_inc(out_ready, 1)

            def restack_scale(g, i):
                m = RG * g + i
                t0 = HT * GROUPS[g][0] + RT * i
                dve.wait_ge(st_raw, m + 1)
                dve.wait_ge(st_lo, m)
                for t in range(RT):
                    last = nc.vector.tensor_scalar(zrow[:, t, :], st_ps[i % 2][:, D * t:D * (t + 1)],
                                                   scale[:, t0 + t:t0 + t + 1], None, ALU.mult)
                last.then_inc(z_ok, 1)

            def restack_low(g, i):
                m = RG * g + i
                t0 = HT * GROUPS[g][0] + RT * i
                dve.wait_ge(st_hi, m + 1)
                if g < 2:
                    lo, hi, rows = xw_lo, xw_hi, st_ps[i % 2].rearrange("p (t d) -> p t d", t=RT)
                else:
                    lo, hi, rows = stat_lo, stat_hi, zrow
                nc.vector.tensor_tensor(lo[:, t0:t0 + RT, :], rows[:, :, :], hi[:, t0:t0 + RT, :].bitcast(f32),
                                        ALU.subtract).then_inc(st_lo, 1)

            def plan_of(after, g):
                if not after:
                    return []
                a, k = after
                first, second = (4, 5) if a < g else (6, 8)
                plan = []
                if a < 2:
                    c = GC * a + k
                    plan = [(first, lambda: rows_first(c)), (second, lambda: rows_second(c))]
                elif a == 2:
                    plan = [(0 if a < g else 4, lambda: add_y(k))]
                elif a == 3:
                    plan = [(7, lambda: add_part(k))]
                else:
                    plan = [(6, lambda: rows_out(a, k))]
                if a < g and a < 4:
                    at_scale = (None, None, (0, 2, 4, 6), (8, 10, 12, 13))[a]
                    at_low = ((9, 10, 12, 14), (9, 10, 12, 14), (0, 2, 4, 6), (9, 11, 13, 14))[a]
                    for i in range(RG):
                        if a > 1:
                            plan += [(at_scale[i], lambda i=i: restack_scale(a, i))]
                        plan += [(at_low[i], lambda i=i: restack_low(a, i))]
                return plan

            turn(0, 0)
            end_of_attention()

            def chunk(g, k, after):
                plan = plan_of(after, g)
                for i, (vg, vk, j) in enumerate(visits(g, k)):
                    v = visit_number(vg, vk, j)
                    for u in range(UNITS):
                        ahead(after, plan, UNITS * i + u)
                        if u < UNITS - 1:
                            turn(v, u + 1)
                        elif not (g == len(GROUPS) - 1 and isinstance(k, int) and k == GC - 1):
                            turn(v + 1, 0)
                        if not is_whole(vg, vk, j, u):
                            low(vg, vk, j, v, u)

            def flush(after):
                rows_out(*after)
            last = None
            for g in range(len(GROUPS)):
                chunk(g, 0, last)
                end = GC if g < len(GROUPS) - 1 else GC - 1
                with dve.Fori(1, end) as k:
                    chunk(g, k, (g, k - 1))
                if end < GC:
                    chunk(g, GC - 1, (g, GC - 2))
                last = (g, GC - 1)
            flush(last)

        @block.scalar
        def _(act):
            start_counts(act, "scalar")
            act.wait_ge(ident_ok, 2)
            act.wait_ge(var_ok, 1)
            nc.scalar.activation(mom[:, 0, :], mom[:, 5, :], ACT.Sqrt, bias=eps_sb[:, 0:1]).then_inc(std_ok, 1)
            act.wait_ge(rstd_ok, 1)
            with act.Fori(HT, TILES - 7, 8) as t0:
                for t in range(8):
                    nc.scalar.activation(tile_of(xs, t0 + t), tile_of(xs, t0 + t), ACT.Relu,
                                         scale=mom[:, 1, at(t0 + t, 1)], bias=mom[:, 3, at(t0 + t, 1)])\
                      .then_inc(h_low, 1)
            act.wait_ge(h_low, HT)
            G = TILES // 4
            for g in range(4):
                if g < 2:
                    act.wait_ge(h_ok, g + 1)
                nc.scalar.activation(stat_hi[:, G * g:G * (g + 1), :], xs[:, G * g:G * (g + 1), :],
                                     ACT.Copy).then_inc(stat_done, 1)
            for g in range(TILES // 4):
                act.wait_ge(hT_ps, g + 1)
                hi = key_columns(keyT_hi, g)
                ps = one[2 + g % 4].rearrange("p (b q s) -> p b q s", b=4, q=NQ)
                nc.scalar.activation(hi, ps, ACT.Copy).then_inc(key_hi_ok, 1)

            def q_part(c):
                wait(act, q_raw, c + 1)
                wait(act, sco_raw, SUNITS * c)
                nc.scalar.activation(q_hi, q_ps, ACT.Copy).then_inc(qh_ok, 1)

            def exp_piece(c, h, e):
                wait(act, max_ok, c + 1)
                i, t, g = e // (2 * QT), e // 2 % QT, e % 2
                s = scores[:, h, t, HALF * i + SG * g:HALF * i + SG * (g + 1)]
                if e == 0:
                    wait(act, rsum_ok, c - 1)
                nc.scalar.activation(s, s, ACT.Exp, bias=nmax[:, h, t:t + 1], scale=-1.0,
                                     accum_out=rpart[:, h, e:e + 1]).then_inc(exp_ok, PUNITS // EXPS)

            def prob_hi(c, u):
                n = PUNITS * c + u
                wait(act, p_turned, PUNITS + n + 1)
                wait(act, pv_unit, n - NPT + 1)
                nc.scalar.activation(probT[:, u % NPT][:, :, 0, :],
                                     turned_p[u % NPT].rearrange("p (k r) -> p k r", k=PK), ACT.Copy)\
                  .then_inc(pT_hi_ok, 1)

            def bt_part(c, h):
                wait(act, pv_unit, PUNITS * (c + 1))
                wait(act, bt_ok, c)
                nc.scalar.activation(bt_half, pv_ps[h][:, QR:2 * QR], ACT.Copy).then_inc(bt_half_ok, 1)

            def step(c, h, more_scores=True, more_probs=True, before=True):
                for u in range(PUNITS):
                    if u == 0 and more_scores:
                        q_part(c + 2)
                    if u == 1 and before:
                        bt_part(c - 1, 1 - h)
                    if u + HI_AHEAD < PUNITS:
                        prob_hi(c, u + HI_AHEAD)
                    elif more_probs:
                        prob_hi(c + 1, u + HI_AHEAD - PUNITS)
                    if more_probs and u in EXP_AT:
                        exp_piece(c + 1, 1 - h, EXP_AT.index(u))

            q_part(0)
            q_part(1)
            for e in range(EXPS):
                exp_piece(0, 0, e)
            for u in range(HI_AHEAD):
                prob_hi(0, u)
            step(0, 0, before=False)
            with act.Fori(1, QCH - 4, 2) as c:
                step(c, 1)
                step(c + 1, 0)
            step(QCH - 3, 1)
            step(QCH - 2, 0, more_scores=False)
            step(QCH - 1, 1, more_scores=False, more_probs=False)
            bt_part(QCH - 1, 1)

            def take(g, k):
                o = GC * g + k
                wait(act, unit_done, UNITS * (visit_number(g, k, len(GROUPS[g][1]) - 1) + 1))
                src = acc_ps[:, at(512 * (k % 2), 512)]
                if g == 3:
                    wait(act, st_raw, RG * 3)
                    nc.scalar.activation(stacked_rows(yT, k), src.rearrange("p (b s) -> p b s", s=SQ), ACT.Copy)\
                      .then_inc(acc_out, 1)
                    return
                if g < 2:
                    wait(act, rows_raw, o)
                elif g == 2:
                    wait(act, rows_raw, 2 * GC)
                    wait(act, y_ok, k)
                else:
                    wait(act, y_ok, GC)
                    wait(act, rows_raw, 2 * GC + GC * (g - 4) + k)
                nc.scalar.activation(uT[:, :], src, ACT.Copy).then_inc(acc_out, 1)

            def take_early():
                act.wait_ge(xw_raw, 1 + 2 * GC)
                act.wait_ge(unit_done, UNITS * (visit_number(3, 0, 0) + 1))
                nc.scalar.activation(h2T[:, :], dual_ps[:, 0:512], ACT.Copy).then_inc(early_ok, 1)

            def take_dual(g, k):
                src = dual_ps[:, at(512 * (k % 2), 512)]
                if g == 1:
                    dst, src = stacked_rows(yT, k), src.rearrange("p (b s) -> p b s", s=SQ)
                else:
                    dst = h2T[:, :]
                    wait(act, xw_raw, 2 * GC)
                    wait(act, part_raw, k)
                wait(act, unit_done, UNITS * (visit_number(g, k, len(GROUPS[g][1]) - 1) + 1))
                nc.scalar.activation(dst, src, ACT.Copy).then_inc(dual_out, 1)

            ov = out.rearrange("(c t p) d -> c p t d", t=CT, p=P)

            def store(g, k):
                wait(act, out_ready, GC * (g - 4) + k + 1)
                nc.scalar.dma_start(ov[at(GC * GROUPS[g][0] + k, 1)].rearrange("c p t d -> (c p) t d"),
                                    outb[:, :, :]).then_inc(stored, 16)

            def std2(c):
                wait(act, var2_ok, c + 1)
                nc.scalar.activation(mom[:, 0, 0:CT], mom[:, 5, 0:CT], ACT.Sqrt, bias=eps_sb[:, 0:1]).then_inc(std2_ok, 1)

            def relu_out(c):
                wait(act, h2_raw, c + 1)
                wait(act, xw_raw, c)
                nc.scalar.activation(h2T[:, :], h2_ps, ACT.Relu).then_inc(h2T_ok, 1)

            def take_xw(g, k):
                wait(act, xw_raw, GC * g + k + 1)
                if g == 1:
                    wait(act, st_raw, RG)
                nc.scalar.activation(stacked_rows(xwT, k), xw_ps.rearrange("p (b s) -> p b s", s=SQ), ACT.Copy)\
                  .then_inc(xw_out, 1)

            def restack(g, i):
                m = RG * g + i
                half = GROUPS[g][0]
                t0 = HT * half + RT * i
                rows = st_ps[i % 2].rearrange("p (t d) -> p t d", t=RT) if g < 2 else zrow
                if g < 2:
                    act.wait_ge(st_raw, m + 1)
                else:
                    act.wait_ge(z_ok, m - 2 * RG + 1)
                for w, u in enumerate(WHOLE):
                    if UT * u // RT == i and g > 0:
                        t = UT * u - RT * i
                        nc.scalar.activation((xw_whole if g < 2 else z_whole)[half][:, UT * w:UT * (w + 1), :],
                                             rows[:, t:t + UT, :], ACT.Copy)
                if g < 2:
                    nc.scalar.activation(xw_hi[:, t0:t0 + RT, :], st_ps[i % 2].rearrange("p (t d) -> p t d", t=RT),
                                         ACT.Copy).then_inc(st_hi, 1)
                else:
                    nc.scalar.activation(stat_hi[:, t0:t0 + RT, :], zrow[:, :, :], ACT.Copy).then_inc(st_hi, 1)

            def plan_of(after, g):
                if not after:
                    return []
                a, k = after
                c = GC * a + k
                if a < 2:
                    at_take, at_std, at_relu, at_xw = (2, 4, 6, 7) if a < g else (3, 7, 11, 13)
                    plan = [(at_take, lambda: take(a, k))]
                    if a == 1:
                        plan += [(at_take, lambda: take_dual(a, k))]
                    plan += [(at_std, lambda: std2(c)), (at_relu, lambda: relu_out(c)), (at_xw, lambda: take_xw(a, k))]
                elif a == 2:
                    plan = [(0 if a < g else 3, lambda: take(a, k))]
                elif a == 3:
                    plan = [(3, lambda: take(a, k)), (3, lambda: take_dual(a, k))]
                else:
                    plan = [(3, lambda: take(a, k)), (7, lambda: store(a, k))]
                if a < g and a < 4:
                    at_restack = ((8, 9, 11, 13), (8, 9, 11, 13), (0, 2, 4, 6), (8, 10, 12, 13))[a]
                    plan += [(at_restack[i], lambda i=i: restack(a, i)) for i in range(RG)]
                if a == 1 and a < g:
                    plan += [(12, take_early)]
                return plan

            def chunk(g, k, after):
                plan = plan_of(after, g)
                for i, (vg, vk, j) in enumerate(visits(g, k)):
                    for u in range(UNITS):
                        ahead(after, plan, UNITS * i + u)
                        if is_whole(vg, vk, j, u):
                            continue
                        n = UNITS * visit_number(vg, vk, j) + u
                        wait(act, adj_turned, n + 1)
                        wait(act, unit_done, n - NH + 1)
                        nc.scalar.activation(adj_hi[u % NH], turned[u % NT], ACT.Copy)\
                          .then_inc(hi_ok, split_count(vg, vk, j, u))

            def flush(after):
                take(*after)
                store(*after)
            passes(act, chunk, flush)

        @block.tensor
        def _(pe):
            start_counts(pe, "tensor")
            mm, tr = nc.tensor.matmul, nc.tensor.transpose
            pe.wait_ge(ident_ok, 2)
            pe.wait_ge(w_in, 16 * W_LOADS)
            for i, w in enumerate((wl_sb, wr_sb, wh_sb)):
                last = tr(one[0][:, D * i:D * (i + 1)], w, ident[:, :])
            last.then_inc(pe_setup, 1)
            for g in range(TILES // 4):
                if g < TILES // 8:
                    pe.wait_ge(h_ok, g // 2 + 1)
                else:
                    pe.wait_ge(h_low, HT)
                wait(pe, keyT_done, g - 3)
                for b in range(4):
                    last = tr(one[2 + g % 4][:, P * b:P * (b + 1)], xs[:, 4 * g + b, :], ident[:, :])
                last.then_inc(hT_ps, 1)
                if g == 1:
                    pe.wait_ge(products_ok, 1)
                    pe.wait_ge(srow_ok, 1)
                    mm(one[1][:, 0:D], wT[:, 0, :], wT[:, 1, :], start=True, stop=True)
                    mm(one[1][:, D:2 * D], wT[:, 2, :], wg_sb, start=True, stop=True)
                    tr(one[1][:, 2 * D:2 * D + TILES], srow, ident[0:TILES, 0:TILES]).then_inc(pe_setup, 1)

            def queries(c):
                wait(pe, q_split, c)
                k_hi, k_lo = keyT_hi[:, at(QR * c, QR)], keyT_lo[:, at(QR * c, QR)]
                mm(q_ps, g_hi[:, :], k_hi, start=True, stop=False)
                mm(q_ps, g_hi[:, :], k_lo, start=False, stop=False)
                mm(q_ps, g_lo[:, :], k_hi, start=False, stop=True).then_inc(q_raw, 1)

            def score_unit(c, u):
                if u == 0:
                    wait(pe, q_split, c + 1)
                wait(pe, sco_out, SUNITS * c + u - 1)
                t, g = u // (N // SG), u % (N // SG)
                for a, k, s, e in ((q_hi, keyT_hi, True, False), (q_hi, keyT_lo, False, False),
                                   (q_lo, keyT_hi, False, True)):
                    for j in range(2):
                        col = SG * g + 512 * j
                        last = mm(sco_ps[u % 2][:, 512 * j:512 * (j + 1)], a[:, P * t:P * (t + 1)],
                                  k[:, col:col + 512], start=s, stop=e)
                last.then_inc(sco_raw, 1)

            def prob_use(c, h, u):
                wait(pe, pT_ok, PUNITS * c + u + 1)
                if isinstance(c, int) and c >= QCH - 2:
                    wait(pe, pT_dve, PUNITS * (c - (QCH - 2)) + u + 1)
                if u == 0:
                    wait(pe, bt_ok, c - 1)
                for k in range(PK):
                    b = PK * u + k
                    s = probT[:, u % NPT, k]
                    both = s.rearrange("p h r -> p (h r)")
                    if b == 0:
                        mm(pv_ps[h], stat_hi[:, b, :], both, start=True, stop=False)
                        last = mm(pv_ps[h][:, 0:QR], stat_lo[:, b, :], s[:, 0, :], start=False, stop=False)
                    else:
                        mm(pv_ps[h][:, 0:QR], stat_lo[:, b, :], s[:, 0, :], start=False, stop=False)
                        last = mm(pv_ps[h], stat_hi[:, b, :], both, start=False, stop=b == TILES - 1)
                last.then_inc(pv_unit, 1)

            def att_rows(c):
                wait(pe, bt_ok, c + 1)
                wait(pe, att_ok, c)
                for t in range(QT):
                    last = mm(att_ps[:, D * t:D * (t + 1)], btT[:, P * t:P * (t + 1)], whg[:, :], start=True, stop=True)
                last.then_inc(att_raw, 1)

            pe.wait_ge(products_ok, 2)
            pe.wait_ge(keyT_done, TILES // 4)
            for c in range(2):
                queries(c)
                for u in range(SUNITS):
                    score_unit(c, u)
            queries(2)

            def step(c, h, more_scores=True, more_queries=True, before=True):
                for u in range(PUNITS):
                    if u == 6 and before:
                        att_rows(c - 1)
                    prob_use(c, h, u)
                    if u in SCORE_AT and more_scores:
                        score_unit(c + 2, SCORE_AT.index(u))
                if more_queries:
                    queries(c + 3)

            step(0, 0, before=False)
            with pe.Fori(1, QCH - 4, 2) as c:
                step(c, 1)
                step(c + 1, 0)
            step(QCH - 3, 1, more_queries=False)
            step(QCH - 2, 0, more_scores=False, more_queries=False)
            step(QCH - 1, 1, more_scores=False, more_queries=False)
            att_rows(QCH - 1)

            stats_of = ((stat_hi, stat_lo), (stat_hi, stat_lo), (xw_hi, xw_lo), (xw_hi, xw_lo),
                        (stat_hi, stat_lo), (stat_hi, stat_lo))
            whole_of = (h_whole, h_whole, xw_whole, xw_whole, z_whole, z_whole)
            new_tiles = {(1, 1): 0, (2, 0): 1, (3, 1): 2, (4, 1): 3}
            whole_made = {(0, 0): 0, (0, 1): 2}
            dual_stats_of = {1: (xw_hi, xw_lo), 3: (stat_hi, stat_lo)}

            def unit(g, k, j, u, acc, dual):
                n = UNITS * visit_number(g, k, j) + u
                cols = GROUPS[g][1]
                whole = is_whole(g, k, j, u)
                if whole:
                    wait(pe, adj_turned, n + 1)
                    if isinstance(k, int) and (g, j) in whole_made:
                        wait(pe, whole_ok, whole_made[g, j] + WHOLE.index(u) + 1)
                else:
                    wait(pe, lo_pool, n + 1)
                    wait(pe, lo_dve, n + 1)
                if isinstance(k, int) and k == 0 and (g, j) in new_tiles:
                    wait(pe, st_lo, RG * new_tiles[g, j] + UT * u // RT + 1)
                for b in range(UT):
                    t = HT * cols[j] + UT * u + b
                    if whole:
                        w = UT * WHOLE.index(u) + b
                        last = mm(acc, whole_of[g][cols[j]][:, w, :], turned[u % NT][:, ROWS * b:ROWS * (b + 1)],
                                  start=False, stop=False)
                        continue
                    hi, lo = adj_hi[u % NH][:, ROWS * b:ROWS * (b + 1)], adj_lo[u % NL][:, ROWS * b:ROWS * (b + 1)]
                    begin, end = u == 0 and b == 0, u == UNITS - 1 and b == UT - 1
                    if dual is not None:
                        s_hi, s_lo = dual_stats_of[g]
                        mm(dual, s_hi[:, t, :], hi, start=begin, stop=False)
                        mm(dual, s_hi[:, t, :], lo, start=False, stop=False)
                        mm(dual, s_lo[:, t, :], hi, start=False, stop=end)
                    s_hi, s_lo = stats_of[g]
                    mm(acc, s_hi[:, t, :], hi, start=begin and j == 0, stop=False)
                    mm(acc, s_hi[:, t, :], lo, start=False, stop=False)
                    last = mm(acc, s_lo[:, t, :], hi, start=False, stop=end and (j == len(cols) - 1 or is_early(g, k, j)))
                last.then_inc(unit_done, 1)

            def sum_rows(g, k):
                wait(pe, acc_out, GC * g + k + 1)
                if g < 2:
                    wait(pe, rows_ok, GC * g + k)
                else:
                    wait(pe, out_ready, GC * (g - 4) + k)
                for t in range(CT):
                    last = tr(row_ps[:, P * t:P * (t + 1)], uT[:, P * t:P * (t + 1)], ident[:, :])
                last.then_inc(rows_raw, 1)

            def part_rows(k):
                wait(pe, dual_out, GC + k + 1)
                wait(pe, part_ok, k)
                for t in range(CT):
                    last = tr(h2_ps[:, P * t:P * (t + 1)], h2T[:, P * t:P * (t + 1)], ident[:, :])
                last.then_inc(part_raw, 1)

            def norm_cols(c):
                wait(pe, hn_ok, c + 1)
                wait(pe, h2T_ok, c)
                for t in range(CT):
                    last = tr(h2_ps[:, P * t:P * (t + 1)], hn[:, t, :], ident[:, :])
                last.then_inc(h2_raw, 1)

            def times_weight(c):
                if isinstance(c, int) and c == 0:
                    pe.wait_ge(late_in, 16 * LATE_LOADS)
                wait(pe, h2T_ok, c + 1)
                wait(pe, xw_out, c)
                mm(xw_ps, w1_sb[:, :], h2T[:, :], start=True, stop=True).then_inc(xw_raw, 1)

            def restack(g, i):
                m = RG * g + i
                if i == 0:
                    if g < 2:
                        wait(pe, xw_out, GC * (g + 1))
                    elif g == 2:
                        wait(pe, y_ok, GC)
                    else:
                        wait(pe, acc_out, 4 * GC)
                wait(pe, st_lo, m - 1)
                for t in range(RT):
                    last = tr(st_ps[i % 2][:, P * t:P * (t + 1)], stacked(xwT if g < 2 else yT, RT * i + t), ident[:, :])
                last.then_inc(st_raw, 1)

            def plan_of(after, g):
                if not after:
                    return []
                a, k = after
                c = GC * a + k
                plan = []
                if a < 2:
                    at_rows, at_norm, at_weight = (2, 5, 6) if a < g else (3, 8, 11)
                    plan = [(at_rows, lambda: sum_rows(a, k)), (at_norm, lambda: norm_cols(c)),
                            (at_weight, lambda: times_weight(c))]
                elif a == 3:
                    plan = [(5, lambda: part_rows(k))]
                elif a > 3:
                    plan = [(4, lambda: sum_rows(a, k))]
                if a < g and a < 4:
                    at_restack = ((7, 8, 9, 11), (7, 8, 9, 11), (0, 0, 2, 4), (5, 6, 8, 10))[a]
                    plan += [(at_restack[i], lambda i=i: restack(a, i)) for i in range(RG)]
                return plan

            def chunk(g, k, after):
                plan = plan_of(after, g)
                acc = acc_ps[:, at(512 * (k % 2), 512)]
                wait(pe, acc_out, GC * g + k - 1)
                for i, (vg, vk, j) in enumerate(visits(g, k)):
                    dual, to = None, acc
                    if DUAL[vg][j]:
                        dual = dual_ps[:, at(512 * (k % 2), 512)]
                        wait(pe, dual_out, GC * (g // 2) + k - 1)
                    if is_early(vg, vk, j):
                        to = dual_ps[:, 0:512]
                        wait(pe, dual_out, GC - 1)
                    elif isinstance(k, int) and (g, k) == (3, 0):
                        pe.wait_ge(whole_ok, 6)
                        pe.wait_ge(early_ok, 1)
                        mm(acc, ident[:, :], h2T[:, :], start=True, stop=False)
                    for u in range(UNITS):
                        ahead(after, plan, UNITS * i + u)
                        unit(vg, vk, j, u, to, dual)
            passes(pe, chunk, lambda after: sum_rows(*after))


_INS = ['x', 'adj', 'L0_gnn_W_l', 'L0_gnn_W_r', 'L0_gnn_W_h', 'L0_gnn_W_g', 'L0_gnn_gamma', 'L1_gnn_d_list',
        'L1_gnn_weight', 'L1_gnn_filt', 'L1_gnn_bias']
_OUTS = [((4096, 128), 'float32')]


def kernel(**inputs):
    import numpy as _np
    import concourse.bacc as _bacc
    from concourse import mybir as _mybir
    from concourse.bass_utils import run_bass_kernel_spmd as _run

    nc = _bacc.Bacc("TRN2", target_bir_lowering=False, num_devices=1)
    arrays, args = {}, []
    for name in _INS:
        a = _np.ascontiguousarray(inputs[name])
        arrays[f"in_{name}_dram"] = a
        args.append(nc.dram_tensor(f"in_{name}_dram", a.shape, _mybir.dt.from_np(a.dtype), kind="ExternalInput").ap())
    for i, (shape, dtype) in enumerate(_OUTS):
        dt = _mybir.dt.from_np(_np.dtype(dtype))
        args.append(nc.dram_tensor(f"out_{i}_dram", shape, dt, kind="ExternalOutput").ap())
    preln_attention_graph_kernel(nc, *args)
    r = _run(nc, [arrays], core_ids=[0])
    return r.results[0]["out_0_dram"]
```
